# Optimizing a Trainium2 kernel written in Bass

```python
import numpy as np
import jax
import jax.numpy as jnp

def _softmax(x, axis=-1):
    return jax.nn.softmax(x, axis=axis)

def _gelu(x):
    return jax.nn.gelu(x, approximate=True)

def _silu(x):
    return jax.nn.silu(x)

def _sigmoid(x):
    return jax.nn.sigmoid(x)

def _layernorm(x, axis=-1, eps=1e-05):
    m = jnp.mean(x, axis=axis, keepdims=True)
    v = jnp.var(x, axis=axis, keepdims=True)
    return (x - m) / jnp.sqrt(v + eps)

def _scatter_add(tgt, idx, src, axis=0):
    return tgt.at[idx].add(src)

def _segment_sum(src, seg, n):
    return jax.ops.segment_sum(src, seg, n)
kernel_name = 'mk_macaron_d1_jaxref_r8_663ae5'

def setup_inputs(seed: int=0):
    np.random.seed(seed)
    _w = jnp.asarray

    def _L0_attn_setup():
        import jax, jax.numpy as jnp
        import numpy as np
        import math
        DIM_EMB = 128
        DIM_QK = 128
        DIM_V = 128
        NORM_FACT = 1.0 / math.sqrt(DIM_EMB)
        key = jax.random.key(seed)
        k0, k1, k2, k3 = jax.random.split(key, 4)
        x = jax.random.normal(k0, (4, 512, DIM_EMB), dtype=jnp.float32)
        s = 1.0 / math.sqrt(DIM_EMB)
        Wq = jax.random.uniform(k1, (DIM_QK, DIM_EMB), jnp.float32, -s, s)
        Wk = jax.random.uniform(k2, (DIM_QK, DIM_EMB), jnp.float32, -s, s)
        Wv = jax.random.uniform(k3, (DIM_V, DIM_EMB), jnp.float32, -s, s)
        return {'x': x, 'Wq': Wq, 'Wk': Wk, 'Wv': Wv}
    _L0_attn_in = _L0_attn_setup()

    def _L0_ffn_setup():
        import jax, jax.numpy as jnp
        import numpy as np
        TOP_K = 8
        key = jax.random.key(seed)
        ks = jax.random.split(key, 6)
        B, S, D, F, E = (2, 128, 128, 64, 64)
        x = jax.random.normal(ks[0], (B, S, D), dtype=jnp.float32)
        centroids = jax.random.normal(ks[1], (E, D), dtype=jnp.float32) * 0.05
        expert_biases = jnp.zeros((E,), dtype=jnp.float32)
        Ws_up = jax.random.normal(ks[2], (D, F), dtype=jnp.float32) / np.sqrt(D)
        Ws_down = jax.random.normal(ks[3], (F, D), dtype=jnp.float32) / np.sqrt(F)
        W_up = jax.random.normal(ks[4], (E, D, F), dtype=jnp.float32) / np.sqrt(D)
        W_down = jax.random.normal(ks[5], (E, F, D), dtype=jnp.float32) / np.sqrt(F)
        return {'x': x, 'centroids': centroids, 'expert_biases': expert_biases, 'Ws_up': Ws_up, 'Ws_down': Ws_down, 'W_up': W_up, 'W_down': W_down}
    _L0_ffn_in = _L0_ffn_setup()
    _d = {'L0_attn_x': _L0_attn_in['x'], 'L0_attn_Wq': _L0_attn_in['Wq'], 'L0_attn_Wk': _L0_attn_in['Wk'], 'L0_attn_Wv': _L0_attn_in['Wv'], 'L0_ffn_centroids': _L0_ffn_in['centroids'], 'L0_ffn_expert_biases': _L0_ffn_in['expert_biases'], 'L0_ffn_Ws_up': _L0_ffn_in['Ws_up'], 'L0_ffn_Ws_down': _L0_ffn_in['Ws_down'], 'L0_ffn_W_up': _L0_ffn_in['W_up'], 'L0_ffn_W_down': _L0_ffn_in['W_down']}
    _x0 = _d['L0_attn_x']
    _d['L0_attn_x'] = jax.random.normal(jax.random.fold_in(jax.random.key(seed), 1), (1, 2048, 128), dtype=_x0.dtype)
    del _x0
    return _d

def reference(L0_attn_x, L0_attn_Wq, L0_attn_Wk, L0_attn_Wv, L0_ffn_centroids, L0_ffn_expert_biases, L0_ffn_Ws_up, L0_ffn_Ws_down, L0_ffn_W_up, L0_ffn_W_down):

    def _L0_attn_ref(x, Wq, Wk, Wv):
        import jax, jax.numpy as jnp
        import numpy as np
        import math
        DIM_EMB = 128
        DIM_QK = 128
        DIM_V = 128
        NORM_FACT = 1.0 / math.sqrt(DIM_EMB)
        q = jnp.einsum('bne,de->bnd', x, Wq)
        k = jnp.einsum('bne,de->bnd', x, Wk)
        v = jnp.einsum('bne,de->bnd', x, Wv)
        logits = jnp.einsum('bnd,bmd->bnm', q, k)
        score = jax.nn.softmax(logits, axis=-1) * NORM_FACT
        att = jnp.einsum('bnm,bmv->bnv', score, v)
        return att

    def _L0_ffn_ref(x, centroids, expert_biases, Ws_up, Ws_down, W_up, W_down):
        import jax, jax.numpy as jnp
        import numpy as np
        TOP_K = 8
        B, S, D = x.shape
        E = centroids.shape[0]
        T = B * S
        xf = x.reshape(T, D)
        shared = jax.nn.silu(xf @ Ws_up) @ Ws_down
        aff = xf @ centroids.T
        biased = aff + expert_biases
        _, idx = jax.lax.top_k(biased, TOP_K)
        sel = jnp.take_along_axis(aff, idx, axis=1)
        w = jax.nn.sigmoid(sel)
        w = w / (jnp.sum(w, axis=-1, keepdims=True) + 1e-08)
        cw = jnp.zeros((T, E), dtype=x.dtype).at[jnp.arange(T)[:, None], idx].add(w)
        h = jax.nn.silu(jnp.einsum('td,edf->etf', xf, W_up))
        y = jnp.einsum('etf,efd->etd', h, W_down)
        routed = jnp.einsum('etd,te->td', y, cw)
        return (shared + routed).reshape(B, S, D)
    x = L0_attn_x
    x = x + 0.5 * _L0_ffn_ref(_layernorm(x, axis=-1), L0_ffn_centroids, L0_ffn_expert_biases, L0_ffn_Ws_up, L0_ffn_Ws_down, L0_ffn_W_up, L0_ffn_W_down)
    x = x + _L0_attn_ref(_layernorm(x, axis=-1), L0_attn_Wq, L0_attn_Wk, L0_attn_Wv)
    x = x + 0.5 * _L0_ffn_ref(_layernorm(x, axis=-1), L0_ffn_centroids, L0_ffn_expert_biases, L0_ffn_Ws_up, L0_ffn_Ws_down, L0_ffn_W_up, L0_ffn_W_down)
    return x

_drawn_inputs = setup_inputs


def setup_inputs(seed=0):
    import zlib

    import numpy as np

    out = dict(_drawn_inputs(seed))
    spreads = {'L0_ffn_expert_biases': (0.0, 0.1)}
    factors = {}
    for name, (base, spread) in spreads.items():
        noise = np.random.default_rng([zlib.crc32(name.encode()), seed]).standard_normal(out[name].shape)
        drawn = base * np.exp(spread * noise) if base else spread * noise
        out[name] = jnp.asarray(drawn.astype(out[name].dtype))
    for name, factor in factors.items():
        out[name] = (out[name] * factor).astype(out[name].dtype)
    return out
```

```python
from contextlib import ExitStack

import concourse.bass as bass
from concourse import mybir

F32 = mybir.dt.float32
F32R = mybir.dt.float32r
ALU = mybir.AluOpType
ACT = mybir.ActivationFunctionType
AX = mybir.AxisListType.X

P = 128
CH = 512
TPC = CH // P
EPS = 1e-5
TOP = 8
LAG = 3
NS, NG, NGP = 3, 3, 4
GT = 2
LOWEST = -3.4e38
TINY = 1e-15


def macaron_kernel(nc, x_d, wup_d, wdn_d, wsup_d, wsdn_d, cent_d, bias_d, wq_d, wk_d, wv_d, out_d):
    T, D = x_d.shape
    E = cent_d.shape[1]
    F = wsup_d.shape[1]
    assert D == P and 2 * F == P and 2 * E == P and T % CH == 0
    NT = T // P
    NCH = T // CH
    PAIRS = E // 2
    UNITS = PAIRS + 1
    NQ = NT // GT
    GW = GT * P
    KB = T // CH
    NORM = 1.0 / float(D) ** 0.5
    WP = 8
    PW = E * F // WP
    SP = 4

    x_v = x_d.rearrange("(t p) d -> p t d", p=P)
    out_v = out_d.rearrange("(t p) d -> p t d", p=P)

    with ExitStack() as ctx:
        def sb(name, shape, dt=F32, stack=ctx):
            return stack.enter_context(nc.sbuf_tensor(name, shape, dt))

        def sem(name):
            return ctx.enter_context(nc.semaphore(name))

        x = sb("x", [P, NT, D])
        ident = sb("ident", [P, P])
        spread = sb("spread", [P, E], F32R)
        wup = [sb("wup_hi", [P, E * F], F32R), sb("wup_lo", [P, E * F], F32R)]
        wdn = [sb("wdn_hi", [P, PAIRS, D], F32R), sb("wdn_lo", [P, PAIRS, D], F32R)]
        qT = [sb("qT_hi", [P, T], F32R), sb("qT_lo", [P, T], F32R)]
        kT = [sb("kT_hi", [P, T], F32R), sb("kT_lo", [P, T], F32R)]
        v = [sb("v_hi", [P, NT, D], F32R), sb("v_lo", [P, NT, D], F32R)]
        SM = E + F + 3 * D
        small = [sb("small_hi", [P, SM], F32R), sb("small_lo", [P, SM], F32R)]
        wsdn = [sb("wsdn_hi", [F, D], F32R), sb("wsdn_lo", [F, D], F32R)]
        bias = sb("bias", [P, E])
        mhalf = sb("mhalf", [P, TPC])
        cen = [s[:, 0:E] for s in small]
        wsup = [s[:, E:E + F] for s in small]
        wq, wk, wv = ([s[:, E + F + i * D:E + F + (i + 1) * D] for s in small] for i in range(3))

        ffn = ctx.enter_context(ExitStack())
        xnT = [sb("xnT_hi", [P, 2, CH], F32R, ffn), sb("xnT_lo", [P, 2, CH], F32R, ffn)]
        x2T = [sb("x2T_hi", [P, CH], F32R, ffn), sb("x2T_lo", [P, CH], F32R, ffn)]
        cwT = sb("cwT", [P, 2, CH], F32R, ffn)
        silu = sb("silu", [P, NS, CH], F32, ffn)
        sel = sb("sel", [P, E, F], F32R, ffn)
        gated = sb("gated", [P, NG, CH], F32, ffn)
        gpart = [sb("gpart_hi", [P, NGP, CH], F32R, ffn), sb("gpart_lo", [P, NGP, CH], F32R, ffn)]
        yT = sb("yT", [P, CH], F32, ffn)
        xn = sb("xn", [P, TPC, D], F32, ffn)
        xn2 = sb("xn2", [P, TPC, D], F32, ffn)
        stat = sb("stat", [P, 2, TPC, 6], F32, ffn)
        mv = sb("mv", [P, 2, TPC, 2], F32, ffn)
        rs = sb("rs", [P, 2, 4, TPC], F32, ffn)
        biased = sb("biased", [P, TPC, E], F32, ffn)
        aff = sb("aff", [P, TPC, E], F32, ffn)
        rec = sb("rec", [P, TPC, E], F32, ffn)
        sil = sb("sil", [P, TPC, E], F32, ffn)
        rest = sb("rest", [P, TPC, E], F32, ffn)
        top = sb("top", [P, TPC, TOP], F32, ffn)
        wsum = sb("wsum", [P, 2, TPC], F32, ffn)
        cw2 = sb("cw2", [P, TPC, 2 * E], F32, ffn)
        raw = sb("raw", [P, 2, PW], F32, ffn)
        raws = sb("raws", [P, SM], F32, ffn)
        rawd = sb("rawd", [F, D], F32, ffn)
        ffn.close()
        pT = [sb("pT_hi", [P, 2, NT, GW], F32R), sb("pT_lo", [P, 2, NT, GW], F32R)]
        prow = sb("prow", [P, T])
        pmax = sb("pmax", [P, KB])
        nmax = sb("nmax", [P, 2])
        psums = sb("psums", [P, NT, 2])
        pinv = sb("pinv", [P, 2, GT, 2])
        oT = sb("oT", [P, GW])

        bank = [ctx.enter_context(nc.psum_tensor(f"bank{i}", [P, CH], F32)) for i in range(4)]
        lrow = ctx.enter_context(nc.psum_tensor("lrow", [P, 4 * CH], F32))
        hid = [lrow[:, 0:CH], lrow[:, CH:2 * CH]]
        gate = [lrow[:, 2 * CH:3 * CH], lrow[:, 3 * CH:4 * CH]]
        yacc = [bank[0], bank[1]]
        mp, mq = bank[2], bank[3]
        tb, ob = [bank[2], bank[3]], [bank[0], bank[1]]

        s_x = [sem(f"x_in{c}") for c in range(NCH)]
        s_small, s_bias = sem("small_in"), sem("bias_in")
        s_raw = [sem("raw_in0"), sem("raw_in1")]
        s_out = sem("out_stored")
        s_pool = sem("pool_step")
        s_id, s_spread = sem("ident_made"), sem("spread_made")
        s_wh, s_wl = sem("small_hi_made"), sem("small_lo_made")
        s_w = sem("weight_piece_split")
        s_sel = sem("sel_piece_made")
        s_hid, s_gate = sem("hidden_ready"), sem("gate_ready")
        s_silu, s_gated = sem("silu_done"), sem("gated_done")
        s_ghi, s_glo = sem("gated_hi_done"), sem("gated_lo_done")
        s_down = sem("down_done")
        s_dve = sem("dve_step")
        p_st, p_rs, p_xn, p_xT, p_hi, p_lo = (sem("p_" + n) for n in ("stats", "rstd", "xn", "xT", "hi", "lo"))
        p_aff, p_affs, p_sil, p_cw, p_cwT, p_cwr = (sem("p_" + n) for n in ("aff", "aff_read", "sil", "cw", "cwT", "cwT_read"))
        e_y, e_yT, e_x, e_st, e_rs, e_xn, e_xT, e_hi, e_lo = (
            sem("e_" + n) for n in ("y", "yT", "x", "stats", "rstd", "xn", "xT", "hi", "lo"))
        e_pr, e_prhi, e_prlo = sem("e_proj"), sem("e_proj_hi"), sem("e_proj_lo")
        a_l, a_mx, a_exp, a_t, a_thi, a_tlo = (sem("a_" + n) for n in ("logits", "max", "exp", "pT", "pT_hi", "pT_lo"))
        a_o, a_oc, a_oT, a_x = (sem("a_" + n) for n in ("o", "o_copied", "oT", "x"))

        block = ctx.enter_context(nc.Block())

        @block.sync
        def _(sp):
            for c in range(NCH):
                sp.dma_start(x[:, c * TPC:(c + 1) * TPC, :], x_v[:, c * TPC:(c + 1) * TPC, :]).then_inc(s_x[c], 16)
                if c == 0:
                    for src, lo, n in ((cent_d, 0, E), (wsup_d, E, F), (wq_d, E + F, D),
                                       (wk_d, E + F + D, D), (wv_d, E + F + 2 * D, D)):
                        sp.dma_start(raws[:, lo:lo + n], src).then_inc(s_small, 16)
                    sp.dma_start(rawd[:, :], wsdn_d).then_inc(s_small, 16)
                    sp.dma_start(bias[:, :], bias_d.partition_broadcast(P)).then_inc(s_bias, 16)
            for k in range(2 * WP):
                if k >= 2:
                    sp.wait_ge(s_w, k - 1)
                src = (wup_d, wdn_d)[k % 2][:, (k // 2) * PW:(k // 2 + 1) * PW]
                sp.dma_start(raw[:, k % 2, :], src).then_inc(s_raw[k % 2], 16)
            for c in range(NCH):
                sp.wait_ge(e_x, NCH + c + 1)
                sp.dma_start(out_v[:, c * TPC:(c + 1) * TPC, :], x[:, c * TPC:(c + 1) * TPC, :]).then_inc(s_out, 16)
            sp.wait_ge(s_out, 16 * NCH)

        @block.gpsimd
        def _(pool):
            steps = [0]

            def link(ins):
                steps[0] += 1
                ins.then_inc(s_pool, 1)
                pool.wait_ge(s_pool, steps[0])

            def rstd(k, n, stats, done):
                pool.wait_ge(stats, n + 1)
                ve, y, t, r = (rs[:, k, i, :] for i in range(4))
                link(nc.gpsimd.tensor_scalar(ve, mv[:, k, :, 1], EPS, None, ALU.add))
                link(nc.gpsimd.tensor_tensor(y, ve, mhalf[:, :], ALU.pow))
                link(nc.gpsimd.tensor_tensor(t, y, y, ALU.mult))
                link(nc.gpsimd.tensor_tensor(t, t, ve, ALU.mult))
                link(nc.gpsimd.tensor_scalar(t, t, -0.5, 1.5, ALU.mult, ALU.add))
                nc.gpsimd.tensor_tensor(r, y, t, ALU.mult).then_inc(done, 1)

            def split_piece(k):
                w = (wup, [w.rearrange("p a d -> p (a d)") for w in wdn])[k % 2]
                at = slice((k // 2) * PW, (k // 2 + 1) * PW)
                pool.wait_ge(s_raw[k % 2], 16 * (k // 2 + 1))
                link(nc.gpsimd.tensor_copy(w[0][:, at], raw[:, k % 2, :]))
                nc.gpsimd.tensor_tensor(w[1][:, at], raw[:, k % 2, :], w[0][:, at].bitcast(F32),
                                        ALU.subtract).then_inc(s_w, 1)

            def make_sel():
                for k in range(SP):
                    at = slice(k * E // SP, (k + 1) * E // SP)
                    nc.gpsimd.tensor_copy(sel[:, at, :], spread[:, at].bitcast(F32).unsqueeze(2)
                                          .to_broadcast([P, E // SP, F])).then_inc(s_sel, 1)

            link(nc.gpsimd.memset(ident[:, :], 0.0))
            nc.gpsimd.affine_select(out=ident[:, :], in_=ident[:, :], compare_op=ALU.not_equal, fill=1.0,
                                    base=0, pattern=[[-1, P]], channel_multiplier=1).then_inc(s_id, 1)
            link(nc.gpsimd.memset(mhalf[:, :], -0.5))
            pool.wait_ge(s_spread, 1)
            make_sel()
            rstd(0, 0, p_st, p_rs)
            split_piece(0)
            split_piece(1)
            rstd(0, 1, p_st, p_rs)
            for k in range(2, 2 * WP):
                split_piece(k)
            for c in range(1, NCH):
                if c + 1 < NCH:
                    rstd(0, c + 1, p_st, p_rs)
                rstd(1, c - 1, e_st, e_rs)
            rstd(1, NCH - 1, e_st, e_rs)
            for c in range(NCH):
                rstd(0, NCH + c, p_st, p_rs)
                if c == 0:
                    make_sel()

        @block.scalar
        def _(act):
            def silu_unit(u, n):
                U = n * UNITS + u
                m = P if u else F
                act.wait_ge(s_hid, U + 1)
                if U >= NS:
                    act.wait_ge(s_gated, U - NS + 1)
                nc.scalar.activation(silu[0:m, U % NS, :], hid[U % 2][0:m, :], ACT.Silu).then_inc(s_silu, 1)

            def hi_unit(u, n):
                U = n * UNITS + u
                m = P if u else F
                act.wait_ge(s_gated, U + 1)
                if U >= NGP:
                    act.wait_ge(s_down, U - NGP + 1)
                nc.scalar.copy(gpart[0][0:m, U % NGP, :], gated[0:m, U % NG, :]).then_inc(s_ghi, 1)

            def pro_hi(n):
                act.wait_ge(p_xT, n + 1)
                nc.scalar.copy(xnT[0][:, n % 2, :], mp[:, :]).then_inc(p_hi, 1)

            def pro_sil(n):
                act.wait_ge(p_affs, n + 1)
                nc.scalar.activation(sil[:, :, :], aff[:, :, :], ACT.Silu).then_inc(p_sil, 1)

            def pro_cwT(n):
                act.wait_ge(p_cwT, n + 1)
                nc.scalar.copy(cwT[:, n % 2, :], mp[:, :]).then_inc(p_cwr, 1)

            def epi_y(n):
                act.wait_ge(s_down, (n + 1) * UNITS)
                if n:
                    act.wait_ge(e_yT, n)
                nc.scalar.mul(yT[:, :], yacc[n % 2][:, :], 0.5).then_inc(e_y, 1)

            def epi_hi(c):
                act.wait_ge(e_xT, c + 1)
                nc.scalar.copy(x2T[0][:, :], mq[:, :]).then_inc(e_hi, 1)

            def epi_proj_hi(c, k):
                act.wait_ge(e_pr, 3 * c + k + 1)
                dst = (qT[0][:, c * CH:(c + 1) * CH], kT[0][:, c * CH:(c + 1) * CH],
                       v[0][:, c * TPC:(c + 1) * TPC, :].rearrange("p t d -> p (t d)"))[k]
                nc.scalar.copy(dst, mq[:, :]).then_inc(e_prhi, 1)

            act.wait_ge(s_small, 16 * 6)
            nc.scalar.copy(small[0][:, :], raws[:, :]).then_inc(s_wh, 1)
            nc.scalar.copy(wsdn[0][:, :], rawd[:, :]).then_inc(s_wh, 1)
            for f in range(2):
                for c in range(NCH):
                    n = f * NCH + c
                    if c == 0:
                        pro_hi(n)
                        pro_sil(n)
                        pro_cwT(n)
                    for u in range(UNITS):
                        silu_unit(u, n)
                        if u or c:
                            hi_unit(*((u - 1, n) if u else (UNITS - 1, n - 1)))
                        if c + 1 < NCH:
                            if u == 8:
                                pro_hi(n + 1)
                            if u == 13:
                                pro_sil(n + 1)
                            if u == 27:
                                pro_cwT(n + 1)
                        if c:
                            if u == 5:
                                epi_y(n - 1)
                            if f == 0 and u == 18:
                                epi_hi(c - 1)
                            if f == 0 and u in (21, 24, 28):
                                epi_proj_hi(c - 1, (21, 24, 28).index(u))
                    if c == NCH - 1:
                        hi_unit(UNITS - 1, n)
                        epi_y(n)
                        if f == 0:
                            epi_hi(c)
                            for k in range(3):
                                epi_proj_hi(c, k)
                if f == 0:
                    def exp_tile(t):
                        act.wait_ge(a_mx, t + 1)
                        for h in range(2):
                            if t:
                                act.wait_ge(a_t, 4 * (t - 1) + 2 * h + 2)
                            nc.scalar.activation(prow[:, h * T // 2:(h + 1) * T // 2], lrow[:, h * T // 2:(h + 1) * T // 2],
                                                 ACT.Exp, bias=nmax[:, t % 2:t % 2 + 1],
                                                 accum_out=psums[:, t, h:h + 1]).then_inc(a_exp, 1)

                    def turn_hi(t):
                        for q in range(4):
                            act.wait_ge(a_t, 4 * t + q + 1)
                            if t // GT >= 2 and t % GT == 0 and q == 0:
                                act.wait_ge(a_o, t // GT - 1)
                            nc.scalar.copy(pT[0][:, t // GT % 2, 4 * q:4 * q + 4, t % GT * P:(t % GT + 1) * P],
                                           tb[q % 2][:, :].rearrange("p (k n) -> p k n", n=P)).then_inc(a_thi, 1)

                    def o_copy(g):
                        act.wait_ge(a_o, g + 1)
                        if g:
                            act.wait_ge(a_oT, g)
                        nc.scalar.copy(oT[:, :], ob[g % 2][:, 0:GW]).then_inc(a_oc, 1)

                    for t in range(NT):
                        exp_tile(t)
                        turn_hi(t)
                        if t % GT == 0 and t // GT >= 2:
                            o_copy(t // GT - 2)
                    o_copy(NQ - 2)
                    o_copy(NQ - 1)

        @block.vector
        def _(dve):
            steps = [0]

            def link(ins):
                steps[0] += 1
                ins.then_inc(s_dve, 1)
                dve.wait_ge(s_dve, steps[0])

            def gate_unit(u, n):
                U = n * UNITS + u
                dve.wait_ge(s_silu, U + 1)
                if U >= NG:
                    dve.wait_ge(s_ghi, U - NG + 1)
                    dve.wait_ge(s_glo, U - NG + 1)
                if u == 0:
                    nc.vector.tensor_copy(gated[0:F, U % NG, :], silu[0:F, U % NS, :]).then_inc(s_gated, 1)
                    return
                R = n * PAIRS + u - 1
                dve.wait_ge(s_gate, R + 1)
                nc.vector.tensor_tensor(gated[:, U % NG, :], silu[:, U % NS, :], gate[R % 2], ALU.mult).then_inc(s_gated, 1)

            def lo_unit(u, n):
                U = n * UNITS + u
                m = P if u else F
                dve.wait_ge(s_ghi, U + 1)
                nc.vector.tensor_tensor(gpart[1][0:m, U % NGP, :], gated[0:m, U % NG, :],
                                        gpart[0][0:m, U % NGP, :].bitcast(F32), ALU.subtract).then_inc(s_glo, 1)

            def stats(k, c, done):
                for i in range(TPC):
                    ins = nc.vector.bn_stats(stat[:, k, i, :], x[:, c * TPC + i, :])
                link(ins)
                for i in range(TPC):
                    ins = nc.vector.bn_aggr(mv[:, k, i, :], stat[:, k, i, :])
                ins.then_inc(done, 1)

            def normed(k, n, c, dst, ready, done):
                dve.wait_ge(ready, n + 1)
                for i in range(TPC):
                    ins = nc.vector.tensor_scalar(dst[:, i, :], x[:, c * TPC + i, :], mv[:, k, i, 0:1],
                                                  rs[:, k, 3, i:i + 1], ALU.subtract, ALU.mult)
                ins.then_inc(done, 1)

            def pro_lo(n):
                dve.wait_ge(p_hi, n + 1)
                nc.vector.tensor_tensor(xnT[1][:, n % 2, :], mp[:, :], xnT[0][:, n % 2, :].bitcast(F32),
                                        ALU.subtract).then_inc(p_lo, 1)

            def bc(ap):
                return ap.unsqueeze(1).to_broadcast([P, TPC, E])

            def pro_aff(n):
                dve.wait_ge(p_aff, n + 1)
                ps = mp[:, 0:TPC * E].rearrange("p (t e) -> p t e", e=E)
                nc.vector.tensor_tensor(biased[:, :, :], ps, bc(bias[:, :]), ALU.add)
                link(nc.vector.tensor_copy(rest[:, :, :], ps))
                link(nc.vector.tensor_tensor(rec[:, :, :], rest[:, :, :], ps, ALU.mult))
                link(nc.vector.tensor_scalar(rec[:, :, :], rec[:, :, :], TINY * TINY, 2 * TINY, ALU.is_lt, ALU.mult))
                nc.vector.tensor_tensor(aff[:, :, :], rec[:, :, :], ps, ALU.add).then_inc(p_affs, 1)

            def pro_top(n, i):
                link(nc.vector.max(top[:, i, :], biased[:, i, :]))
                ins = nc.vector.match_replace(rest[:, i, :], top[:, i, :], biased[:, i, :], LOWEST)
                if i == TPC - 1:
                    link(ins)

            def pro_w1(n):
                dve.wait_ge(p_affs, n + 1)
                link(nc.vector.reciprocal(rec[:, :, :], aff[:, :, :]))
                link(nc.vector.tensor_tensor(rest[:, :, :], rest[:, :, :], biased[:, :, :], ALU.not_equal))
                link(nc.vector.tensor_tensor(rec[:, :, :], rec[:, :, :], rest[:, :, :], ALU.mult))

            def pro_w2(n):
                dve.wait_ge(p_sil, n + 1)
                link(nc.vector.tensor_tensor(rec[:, :, :], rec[:, :, :], sil[:, :, :], ALU.mult))
                link(nc.vector.tensor_reduce(wsum[:, 0, :], rec[:, :, :], AX, ALU.add))
                link(nc.vector.tensor_scalar(wsum[:, 0, :], wsum[:, 0, :], 1e-8, None, ALU.add))
                link(nc.vector.reciprocal(wsum[:, 1, :], wsum[:, 0, :]))

            def pro_w3(n):
                link(nc.vector.tensor_tensor(rec[:, :, :], rec[:, :, :],
                                             wsum[:, 1, :].unsqueeze(2).to_broadcast([P, TPC, E]), ALU.mult))
                link(nc.vector.tensor_copy(cw2[:, :, 0:E].bitcast(F32R), rec[:, :, :]))
                nc.vector.tensor_tensor(cw2[:, :, E:2 * E], rec[:, :, :], cw2[:, :, 0:E], ALU.subtract).then_inc(p_cw, 1)

            def epi_x(n, c):
                dve.wait_ge(e_yT, n + 1)
                nc.vector.tensor_tensor(x[:, c * TPC:(c + 1) * TPC, :], x[:, c * TPC:(c + 1) * TPC, :],
                                        mq[:, :].rearrange("p (t d) -> p t d", d=D), ALU.add).then_inc(e_x, 1)

            def epi_lo(c):
                dve.wait_ge(e_hi, c + 1)
                nc.vector.tensor_tensor(x2T[1][:, :], mq[:, :], x2T[0][:, :].bitcast(F32), ALU.subtract).then_inc(e_lo, 1)

            def epi_proj_lo(c, k):
                dve.wait_ge(e_prhi, 3 * c + k + 1)
                dst = [(qT[h][:, c * CH:(c + 1) * CH], kT[h][:, c * CH:(c + 1) * CH],
                        v[h][:, c * TPC:(c + 1) * TPC, :].rearrange("p t d -> p (t d)"))[k] for h in range(2)]
                nc.vector.tensor_tensor(dst[1], mq[:, :], dst[0].bitcast(F32), ALU.subtract).then_inc(e_prlo, 1)

            def epi_stats(c):
                dve.wait_ge(e_x, c + 1)
                stats(1, c, e_st)

            dve.wait_ge(s_x[0], 16)
            stats(0, 0, p_st)
            dve.wait_ge(s_id, 1)
            nc.vector.tensor_tensor(spread[:, :], ident[:, 0:E], ident[:, E:2 * E], ALU.add).then_inc(s_spread, 1)
            dve.wait_ge(s_wh, 2)
            nc.vector.tensor_tensor(small[1][:, :], raws[:, :], small[0][:, :].bitcast(F32), ALU.subtract).then_inc(s_wl, 1)
            nc.vector.tensor_tensor(wsdn[1][:, :], rawd[:, :], wsdn[0][:, :].bitcast(F32), ALU.subtract).then_inc(s_wl, 1)
            dve.wait_ge(s_bias, 16)
            for f in range(2):
                for c in range(NCH):
                    n = f * NCH + c
                    if c == 0:
                        if f:
                            stats(0, 0, p_st)
                        normed(0, n, 0, xn, p_rs, p_xn)
                        pro_lo(n)
                        pro_aff(n)
                        for i in range(TPC):
                            pro_top(n, i)
                        pro_w1(n)
                        pro_w2(n)
                        pro_w3(n)
                    for u in range(UNITS):
                        gate_unit(u, n)
                        if u or c:
                            lo_unit(*((u - 1, n) if u else (UNITS - 1, n - 1)))
                        if c + 1 < NCH:
                            if u == 1:
                                if f == 0:
                                    dve.wait_ge(s_x[c + 1], 16)
                                stats(0, c + 1, p_st)
                            if u == 5:
                                normed(0, n + 1, c + 1, xn, p_rs, p_xn)
                            if u == 8:
                                pro_lo(n + 1)
                            if u == 12:
                                pro_aff(n + 1)
                            if 13 <= u < 13 + TPC:
                                pro_top(n + 1, u - 13)
                            if u == 18:
                                pro_w1(n + 1)
                            if u == 20:
                                pro_w2(n + 1)
                            if u == 22:
                                pro_w3(n + 1)
                        if c:
                            if u == 9:
                                epi_x(n - 1, c - 1)
                            if f == 0:
                                if u == 10:
                                    epi_stats(c - 1)
                                if u == 14:
                                    normed(1, c - 1, c - 1, xn2, e_rs, e_xn)
                                if u == 18:
                                    epi_lo(c - 1)
                                if u in (21, 24, 28):
                                    epi_proj_lo(c - 1, (21, 24, 28).index(u))
                    if c == NCH - 1:
                        lo_unit(UNITS - 1, n)
                        epi_x(n, c)
                        if f == 0:
                            epi_stats(c)
                            normed(1, c, c, xn2, e_rs, e_xn)
                            epi_lo(c)
                            for k in range(3):
                                epi_proj_lo(c, k)
                if f == 0:
                    def turn_lo(t, q):
                        dve.wait_ge(a_thi, 4 * t + q + 1)
                        at = (slice(None), t // GT % 2, slice(4 * q, 4 * q + 4), slice(t % GT * P, (t % GT + 1) * P))
                        nc.vector.tensor_tensor(pT[1][at], tb[q % 2][:, :].rearrange("p (k n) -> p k n", n=P),
                                                pT[0][at].bitcast(F32), ALU.subtract).then_inc(a_tlo, 1)

                    def max_bank(t, j):
                        dve.wait_ge(a_l, KB * t + j + 1)
                        return nc.vector.reduce_max(pmax[:, j:j + 1], lrow[:, j * CH:(j + 1) * CH], AX)

                    def row_max(t):
                        if t >= 2:
                            dve.wait_ge(a_exp, 2 * (t - 1))
                        link(nc.vector.reduce_max(nmax[:, t % 2:t % 2 + 1], pmax[:, :], AX))
                        nc.vector.tensor_scalar(nmax[:, t % 2:t % 2 + 1], nmax[:, t % 2:t % 2 + 1], -1.0, None,
                                                ALU.mult).then_inc(a_mx, 1)

                    def inverse(g):
                        link(nc.vector.tensor_reduce(pinv[:, g % 2, :, 0], psums[:, GT * g:GT * (g + 1), :], AX, ALU.add))
                        link(nc.vector.reciprocal(pinv[:, g % 2, :, 1], pinv[:, g % 2, :, 0]))
                        link(nc.vector.tensor_scalar(pinv[:, g % 2, :, 0], pinv[:, g % 2, :, 1], NORM, None, ALU.mult))

                    def add_o(g):
                        dve.wait_ge(a_oT, g + 1)
                        inverse(g)
                        for i in range(GT):
                            ins = nc.vector.scalar_tensor_tensor(
                                out=x[:, GT * g + i, :], in0=ob[g % 2][:, GW + i * P:GW + (i + 1) * P],
                                scalar=pinv[:, g % 2, i, 0:1], in1=x[:, GT * g + i, :], op0=ALU.mult, op1=ALU.add)
                        ins.then_inc(a_x, 1)

                    for t in range(NT):
                        for j in range(KB):
                            if t:
                                turn_lo(t - 1, j)
                            ins = max_bank(t, j)
                        link(ins)
                        row_max(t)
                        if t % GT == 1 and t // GT >= 2:
                            add_o(t // GT - 2)
                    for j in range(KB):
                        turn_lo(NT - 1, j)
                    add_o(NQ - 2)
                    add_o(NQ - 1)
                    dve.wait_ge(a_x, NQ)

        @block.tensor
        def _(pe):
            def product(out, a, b):
                nc.tensor.matmul(out, a[0], b[1], start=True, stop=False)
                nc.tensor.matmul(out, a[1], b[0], start=False, stop=False)
                return nc.tensor.matmul(out, a[0], b[0], start=False, stop=True)

            def up(u, n):
                U = n * UNITS + u
                if n == 0 and u and (u - 1) % (PAIRS // WP) == 0:
                    pe.wait_ge(s_w, 2 * ((u - 1) // (PAIRS // WP)) + 1)
                if U >= 2:
                    pe.wait_ge(s_silu, U - 1)
                w = [a[:, (u - 1) * P:u * P] for a in wup] if u else wsup
                product(hid[U % 2][0:P if u else F, :], w, [a[:, n % 2, :] for a in xnT]).then_inc(s_hid, 1)
                if u:
                    R = n * PAIRS + u - 1
                    if R >= 2:
                        pe.wait_ge(s_gated, n * UNITS + u - 1 if u > 2 else n * UNITS + u - 2)
                    if n % NCH == 0 and (u - 1) % (PAIRS // SP) == 0:
                        pe.wait_ge(s_sel, n // NCH * SP + (u - 1) // (PAIRS // SP) + 1)
                    one = sel[:, 2 * u - 2:2 * u, :].rearrange("p e f -> p (e f)")
                    nc.tensor.matmul(gate[R % 2], one, cwT[:, n % 2, :], start=True, stop=True).then_inc(s_gate, 1)

            def down(u, n):
                U = n * UNITS + u
                m = P if u else F
                if n == 0 and u and (u - 1) % (PAIRS // WP) == 0:
                    pe.wait_ge(s_w, 2 * ((u - 1) // (PAIRS // WP)) + 2)
                if u == 0 and n % NCH >= 2:
                    pe.wait_ge(e_y, n - 1)
                pe.wait_ge(s_glo, U + 1)
                w = [a[:, u - 1, :] for a in wdn] if u else [a[:, :] for a in wsdn]
                g = [a[0:m, U % NGP, :] for a in gpart]
                y = yacc[n % 2][:, :]
                nc.tensor.matmul(y, w[0], g[1], start=(u == 0), stop=False)
                nc.tensor.matmul(y, w[1], g[0], start=False, stop=False)
                nc.tensor.matmul(y, w[0], g[0], start=False, stop=(u == UNITS - 1)).then_inc(s_down, 1)

            def turn(src, ps, done):
                for i in range(TPC):
                    ins = nc.tensor.transpose(ps[:, i * P:(i + 1) * P], src[:, i * P:(i + 1) * P], ident[:, :])
                ins.then_inc(done, 1)

            def flat(t):
                return t[:, :, :].rearrange("p t d -> p (t d)")

            def pro_xT(n):
                pe.wait_ge(p_xn, n + 1)
                if n:
                    pe.wait_ge(p_cwr, n)
                turn(flat(xn), mp, p_xT)

            def pro_aff(n):
                pe.wait_ge(p_lo, n + 1)
                for i in range(TPC):
                    ins = product(mp[:, i * E:(i + 1) * E], [a[:, n % 2, i * P:(i + 1) * P] for a in xnT], cen)
                ins.then_inc(p_aff, 1)

            def pro_cw(n):
                pe.wait_ge(p_cw, n + 1)
                turn(flat(cw2), mp, p_cwT)

            def epi_yT(n):
                pe.wait_ge(e_y, n + 1)
                if 0 < n <= NCH:
                    pe.wait_ge(e_prlo, 3 * n)
                elif n:
                    pe.wait_ge(e_x, n)
                turn(yT, mq, e_yT)

            def epi_xT(c):
                pe.wait_ge(e_xn, c + 1)
                turn(flat(xn2), mq, e_xT)

            def epi_proj(c, k):
                if k == 0:
                    pe.wait_ge(e_lo, c + 1)
                else:
                    pe.wait_ge(e_prlo, 3 * c + k)
                if k < 2:
                    ins = product(mq[:, :], (wq, wk)[k], [a[:, :] for a in x2T])
                else:
                    for i in range(TPC):
                        ins = product(mq[:, i * D:(i + 1) * D], [a[:, i * P:(i + 1) * P] for a in x2T], wv)
                ins.then_inc(e_pr, 1)

            pe.wait_ge(s_id, 1)
            for f in range(2):
                for c in range(NCH):
                    n = f * NCH + c
                    if c == 0:
                        pro_xT(n)
                        if n == 0:
                            pe.wait_ge(s_wl, 2)
                        pro_aff(n)
                        pro_cw(n)
                    pe.wait_ge(p_cwr, n + 1)
                    for u in range(UNITS):
                        up(u, n)
                        if u >= LAG:
                            down(u - LAG, n)
                        elif c:
                            down(UNITS - LAG + u, n - 1)
                        if c + 1 < NCH:
                            if u == 7:
                                pro_xT(n + 1)
                            if u == 11:
                                pro_aff(n + 1)
                            if u == 26:
                                pro_cw(n + 1)
                        if c:
                            if u == 8:
                                epi_yT(n - 1)
                            if f == 0:
                                if u == 17:
                                    epi_xT(c - 1)
                                if u in (20, 23, 27):
                                    epi_proj(c - 1, (20, 23, 27).index(u))
                    if c == NCH - 1:
                        for u in range(UNITS - LAG, UNITS):
                            down(u, n)
                        epi_yT(n)
                        if f == 0:
                            epi_xT(c)
                            for k in range(3):
                                epi_proj(c, k)
                if f == 0:
                    def logits(t, j):
                        if t:
                            pe.wait_ge(a_exp, 2 * (t - 1) + j // 2 + 1)
                        product(lrow[:, j * CH:(j + 1) * CH], [a[:, t * P:(t + 1) * P] for a in qT],
                                [a[:, j * CH:(j + 1) * CH] for a in kT]).then_inc(a_l, 1)

                    def turn_p(t, q):
                        pe.wait_ge(a_exp, 2 * t + q // 2 + 1)
                        if 4 * t + q >= 2:
                            pe.wait_ge(a_tlo, 4 * t + q - 1)
                        turn(prow[:, q * CH:(q + 1) * CH], tb[q % 2], a_t)

                    def weigh(g, h):
                        if h == 0 and g >= 2:
                            pe.wait_ge(a_x, g - 1)
                        for k in range(h * NT // 2, (h + 1) * NT // 2):
                            if k % 4 == 0:
                                pe.wait_ge(a_tlo, 4 * (GT * g + GT - 1) + k // 4 + 1)
                            p = [a[:, g % 2, k, :] for a in pT]
                            o = ob[g % 2][:, 0:GW]
                            nc.tensor.matmul(o, v[0][:, k, :], p[1], start=(k == 0), stop=False)
                            nc.tensor.matmul(o, v[1][:, k, :], p[0], start=False, stop=False)
                            ins = nc.tensor.matmul(o, v[0][:, k, :], p[0], start=False, stop=(k == NT - 1))
                        if h:
                            ins.then_inc(a_o, 1)

                    def turn_o(g):
                        pe.wait_ge(a_oc, g + 1)
                        for i in range(GT):
                            ins = nc.tensor.transpose(ob[g % 2][:, GW + i * P:GW + (i + 1) * P],
                                                      oT[:, i * P:(i + 1) * P], ident[:, :])
                        ins.then_inc(a_oT, 1)

                    pe.wait_ge(e_prlo, 3 * NCH)
                    for t in range(NT):
                        g = t // GT
                        for j in range(KB):
                            if t:
                                turn_p(t - 1, j)
                            logits(t, j)
                        if t % GT == 1 and g >= 2:
                            turn_o(g - 2)
                        if g:
                            weigh(g - 1, t % GT)
                    for j in range(KB):
                        turn_p(NT - 1, j)
                    turn_o(NQ - 2)
                    weigh(NQ - 1, 0)
                    weigh(NQ - 1, 1)
                    turn_o(NQ - 1)


def kernel(L0_attn_x, L0_attn_Wq, L0_attn_Wk, L0_attn_Wv, L0_ffn_centroids, L0_ffn_expert_biases,
           L0_ffn_Ws_up, L0_ffn_Ws_down, L0_ffn_W_up, L0_ffn_W_down):
    import numpy as np
    import concourse.bacc as bacc
    from concourse.bass_utils import run_bass_kernel_spmd as run

    x = np.asarray(L0_attn_x)
    b, s, d = x.shape
    w_up, w_down = np.asarray(L0_ffn_W_up), np.asarray(L0_ffn_W_down)
    e, _, f = w_up.shape
    arrays = {
        "x": x.reshape(b * s, d),
        "w_up": w_up.transpose(1, 0, 2).reshape(d, e * f),
        "w_down": w_down.reshape(e // 2, 2 * f, d).transpose(1, 0, 2).reshape(2 * f, e // 2 * d),
        "ws_up": np.asarray(L0_ffn_Ws_up),
        "ws_down": np.asarray(L0_ffn_Ws_down),
        "centroids": np.asarray(L0_ffn_centroids).T,
        "biases": np.asarray(L0_ffn_expert_biases),
        "wq": np.asarray(L0_attn_Wq).T,
        "wk": np.asarray(L0_attn_Wk).T,
        "wv": np.asarray(L0_attn_Wv).T,
    }
    arrays = {n: np.ascontiguousarray(a) for n, a in arrays.items()}
    nc = bacc.Bacc("TRN2", target_bir_lowering=False, num_devices=1)
    args = [nc.dram_tensor("in_" + n, a.shape, mybir.dt.from_np(a.dtype), kind="ExternalInput").ap() for n, a in arrays.items()]
    out = nc.dram_tensor("out_dram", (b * s, d), F32, kind="ExternalOutput").ap()
    macaron_kernel(nc, *args, out)
    r = run(nc, [{"in_" + n: a for n, a in arrays.items()}], core_ids=[0])
    return r.results[0]["out_dram"].reshape(b, s, d)
```

```python
from contextlib import ExitStack

import concourse.bass as bass
from concourse import mybir

F32 = mybir.dt.float32
F32R = mybir.dt.float32r
ALU = mybir.AluOpType
ACT = mybir.ActivationFunctionType
AX = mybir.AxisListType.X

P = 128
CH = 512
TPC = CH // P
EPS = 1e-5
TOP = 8
LAG = 3
NS, NG, NGP = 3, 3, 4
GT = 2
PRE = 8
LEAD = 3
T_XT, T_AFF = 13, 14
SHARE = (0, 1, 1, 6)
LOWEST = -3.4e38
TINY = 1e-15


def macaron_kernel(nc, x_d, wup_d, wdn_d, wsup_d, wsdn_d, cent_d, bias_d, wq_d, wk_d, wv_d, out_d):
    T, D = x_d.shape
    E = cent_d.shape[1]
    F = wsup_d.shape[1]
    assert D == P and 2 * F == P and 2 * E == P and T % CH == 0
    NT = T // P
    NCH = T // CH
    PAIRS = E // 2
    UNITS = PAIRS + 1
    NQ = NT // GT
    GW = GT * P
    KB = T // CH
    NORM = 1.0 / float(D) ** 0.5
    NR = 4
    WP = 8
    PW = E * F // WP
    SP = 4

    x_v = x_d.rearrange("(t p) d -> p t d", p=P)
    out_v = out_d.rearrange("(t p) d -> p t d", p=P)

    with ExitStack() as ctx:
        def sb(name, shape, dt=F32, stack=ctx):
            return stack.enter_context(nc.sbuf_tensor(name, shape, dt))

        def sem(name):
            return ctx.enter_context(nc.semaphore(name))

        x = sb("x", [P, NT, D])
        ident = sb("ident", [P, P])
        spread = sb("spread", [P, E], F32R)
        wup = [sb("wup_hi", [P, E * F], F32R), sb("wup_lo", [P, E * F], F32R)]
        wdn = [sb("wdn_hi", [P, PAIRS, D], F32R), sb("wdn_lo", [P, PAIRS, D], F32R)]
        early = ctx.enter_context(ExitStack())
        xnT_b = [sb("xnT_hi_b", [P, 2, CH], F32R, early)]
        xn_b, cwT_b1 = sb("xn_b", [P, TPC, D], F32, early), sb("cwT_b1", [P, CH], F32R, early)
        xnT_b.append(sb("xnT_lo_b", [P, 2, CH], F32R, early))
        biased_b, aff_b = sb("biased_b", [P, TPC, E], F32, early), sb("aff_b", [P, TPC, E], F32, early)
        early.close()
        qT = [sb("qT_hi", [P, T], F32R), sb("qT_lo", [P, T], F32R)]
        kT = [sb("kT_hi", [P, T], F32R), sb("kT_lo", [P, T], F32R)]
        v = [sb("v_hi", [P, NT, D], F32R), sb("v_lo", [P, NT, D], F32R)]
        SM = E + F + 3 * D
        small = [sb("small_hi", [P, SM], F32R), sb("small_lo", [P, SM], F32R)]
        wsdn = [sb("wsdn_hi", [F, D], F32R), sb("wsdn_lo", [F, D], F32R)]
        bias = sb("bias", [P, E])
        mhalf = sb("mhalf", [P, TPC])
        cen = [s[:, 0:E] for s in small]
        wsup = [s[:, E:E + F] for s in small]
        wq, wk, wv = ([s[:, E + F + i * D:E + F + (i + 1) * D] for s in small] for i in range(3))

        cwT_0 = sb("cwT_0", [P, CH], F32R)
        stat = sb("stat", [P, 2, TPC, 6])
        mv = sb("mv", [P, 2, TPC, 2])
        rs = sb("rs", [P, 2, 4, TPC])
        rec = sb("rec", [P, TPC, E])
        sil = sb("sil", [P, TPC, E])
        rest = sb("rest", [P, TPC, E])
        top = sb("top", [P, TPC, TOP])
        wsum = sb("wsum", [P, 2, TPC])
        cw2 = sb("cw2", [P, TPC, 2 * E])

        ffn = ctx.enter_context(ExitStack())
        sel = sb("sel", [P, E, F], F32R, ffn)
        xnT_a = [sb("xnT_hi_a", [P, 2, CH], F32R, ffn), sb("xnT_lo_a", [P, 2, CH], F32R, ffn)]
        xn_a, cwT_a1 = sb("xn_a", [P, TPC, D], F32, ffn), sb("cwT_a1", [P, CH], F32R, ffn)
        biased_a, aff_a = sb("biased_a", [P, TPC, E], F32, ffn), sb("aff_a", [P, TPC, E], F32, ffn)
        silu = sb("silu", [P, NS, CH], F32, ffn)
        gated = sb("gated", [P, NG, CH], F32, ffn)
        with ExitStack() as first:
            raws = sb("raws", [P, SM], F32, first)
            rawd = sb("rawd", [F, D], F32, first)
        gpart = [sb("gpart_hi", [P, NGP, CH], F32R, ffn), sb("gpart_lo", [P, NGP, CH], F32R, ffn)]
        with ExitStack() as first:
            raw = sb("raw", [P, NR, PW], F32, first)
        x2T = [sb("x2T_hi", [P, CH], F32R, ffn), sb("x2T_lo", [P, CH], F32R, ffn)]
        yT = sb("yT", [P, CH], F32, ffn)
        xn2 = sb("xn2", [P, TPC, D], F32, ffn)
        ffn.close()
        xnT, xn, cwT = [xnT_a, xnT_b], [xn_a, xn_b], [[cwT_0, cwT_a1], [cwT_0, cwT_b1]]
        biased, aff = [biased_a, biased_b], [aff_a, aff_b]
        pT = [sb("pT_hi", [P, 2, NT, GW], F32R), sb("pT_lo", [P, 2, NT, GW], F32R)]
        prow = sb("prow", [P, T])
        pmax = sb("pmax", [P, KB])
        nmax = sb("nmax", [P, 2])
        psums = sb("psums", [P, NT, KB])
        pinv = sb("pinv", [P, 2, GT, 2])
        oT = sb("oT", [P, GW])

        bank = [ctx.enter_context(nc.psum_tensor(f"bank{i}", [P, CH], F32)) for i in range(4)]
        lrow = ctx.enter_context(nc.psum_tensor("lrow", [P, 4 * CH], F32))
        hid = [lrow[:, 0:CH], lrow[:, CH:2 * CH]]
        gate = [lrow[:, 2 * CH:3 * CH], lrow[:, 3 * CH:4 * CH]]
        yacc = [bank[0], bank[1]]
        mp, mq = bank[2], bank[3]
        tb, ob = [bank[2], bank[3]], [bank[0], bank[1]]

        s_x = [sem(f"x_in{c}") for c in range(NCH)]
        s_small, s_bias = sem("small_in"), sem("bias_in")
        s_raw = [sem(f"raw_in{i}") for i in range(NR)]
        s_out = sem("out_stored")
        s_pool = sem("pool_step")
        s_id, s_spread = sem("ident_made"), sem("spread_made")
        s_wh, s_wl = sem("small_hi_made"), sem("small_lo_made")
        s_whi = sem("weight_piece_hi")
        s_w = sem("weight_piece_split")
        s_sel = sem("sel_piece_made")
        s_hid, s_gate = sem("hidden_ready"), sem("gate_ready")
        s_silu, s_gated = sem("silu_done"), sem("gated_done")
        s_ghi, s_glo, s_glop = sem("gated_hi_done"), sem("gated_lo_done_dve"), sem("gated_lo_done_pool")
        s_down = sem("down_done")
        s_dve = sem("dve_step")
        p_st, p_rs, p_xn, p_xT, p_hi, p_lo = (sem("p_" + n) for n in ("stats", "rstd", "xn", "xT", "hi", "lo"))
        p_aff, p_affs, p_bias, p_max, p_sil, p_top, p_w, p_inv, p_cw, p_cwT, p_cwr = (
            sem("p_" + n) for n in ("aff", "aff_read", "biased", "max", "sil", "top", "w", "inv", "cw", "cwT", "cwT_read"))
        e_y, e_yT, e_x, e_st, e_rs, e_xn, e_xT, e_hi, e_lo = (
            sem("e_" + n) for n in ("y", "yT", "x", "stats", "rstd", "xn", "xT", "hi", "lo"))
        e_pr, e_prhi, e_prlo = sem("e_proj"), sem("e_proj_hi"), sem("e_proj_lo")
        a_l, a_mx, a_exp, a_t, a_thi, a_tlo = (sem("a_" + n) for n in ("logits", "max", "exp", "pT", "pT_hi", "pT_lo"))
        a_o, a_oc, a_oT, a_x = (sem("a_" + n) for n in ("o", "o_copied", "oT", "x"))

        def proj_bank(c, k):
            if c == NCH - 1:
                return (lrow[:, (KB - 1) * CH:KB * CH], bank[0][:, :], bank[1][:, :])[k]
            return (mq, bank[0], mp)[k][:, :] if c == NCH - 2 else mq[:, :]

        def proj_parts(c, k):
            return [(kT[h][:, c * CH:(c + 1) * CH], qT[h][:, c * CH:(c + 1) * CH],
                     v[h][:, c * TPC:(c + 1) * TPC, :].rearrange("p t d -> p (t d)"))[k] for h in range(2)]

        def on_pool(u):
            return u % 2 == 1

        def lows(U, pool):
            units = [u for u in range(UNITS) if on_pool(u) == pool]
            return U // UNITS * len(units) + sum(u <= U % UNITS for u in units)

        def wait_low(eng, U):
            pool = on_pool(U % UNITS)
            eng.wait_ge(s_glop if pool else s_glo, lows(U, pool))

        def flat(t):
            return t[:, :, :].rearrange("p t d -> p (t d)")

        def low_part(eng, U):
            m = P if U % UNITS else F
            eng.wait_ge(s_ghi, U + 1)
            return eng.tensor_tensor(gpart[1][0:m, U % NGP, :], gated[0:m, U % NG, :],
                                     gpart[0][0:m, U % NGP, :].bitcast(F32), ALU.subtract)

        def piece(k, part):
            w = (wup[part], flat(wdn[part]))[k % 2]
            return w[:, (k // 2) * PW:(k // 2 + 1) * PW]

        block = ctx.enter_context(nc.Block())

        @block.sync
        def _(sp):
            def load_x(c):
                sp.dma_start(x[:, c * TPC:(c + 1) * TPC, :], x_v[:, c * TPC:(c + 1) * TPC, :]).then_inc(s_x[c], 16)

            load_x(0)
            for src, lo, n in ((cent_d, 0, E), (wsup_d, E, F), (wq_d, E + F, D),
                               (wk_d, E + F + D, D), (wv_d, E + F + 2 * D, D)):
                sp.dma_start(raws[:, lo:lo + n], src).then_inc(s_small, 16)
            sp.dma_start(rawd[:, :], wsdn_d).then_inc(s_small, 16)
            sp.dma_start(bias[:, :], bias_d.partition_broadcast(P)).then_inc(s_bias, 16)
            for k in range(2 * WP):
                if k >= NR:
                    sp.wait_ge(s_w, k - NR + 1)
                if NR <= k < NR + NCH - 1:
                    load_x(k - NR + 1)
                src = (wup_d, wdn_d)[k % 2][:, (k // 2) * PW:(k // 2 + 1) * PW]
                sp.dma_start(raw[:, k % NR, :], src).then_inc(s_raw[k % NR], 16)
            for c in range(NCH):
                sp.wait_ge(e_x, NCH + c + 1)
                sp.dma_start(out_v[:, c * TPC:(c + 1) * TPC, :], x[:, c * TPC:(c + 1) * TPC, :]).then_inc(s_out, 16)
            sp.wait_ge(s_out, 16 * NCH)

        @block.gpsimd
        def _(pool):
            steps = [0]

            def link(ins):
                steps[0] += 1
                ins.then_inc(s_pool, 1)
                pool.wait_ge(s_pool, steps[0])

            def rstd(k, n, stats, done):
                pool.wait_ge(stats, n + 1)
                ve, y, t, r = (rs[:, k, i, :] for i in range(4))
                link(nc.gpsimd.tensor_scalar(ve, mv[:, k, :, 1], EPS, None, ALU.add))
                link(nc.gpsimd.tensor_tensor(y, ve, mhalf[:, :], ALU.pow))
                link(nc.gpsimd.tensor_tensor(t, y, y, ALU.mult))
                link(nc.gpsimd.tensor_tensor(t, t, ve, ALU.mult))
                link(nc.gpsimd.tensor_scalar(t, t, -0.5, 1.5, ALU.mult, ALU.add))
                nc.gpsimd.tensor_tensor(r, y, t, ALU.mult).then_inc(done, 1)

            def piece_lo(k):
                pool.wait_ge(s_whi, k + 1)
                nc.gpsimd.tensor_tensor(piece(k, 1), raw[:, k % NR, :], piece(k, 0).bitcast(F32), ALU.subtract).then_inc(s_w, 1)

            def weights(n):
                pool.wait_ge(p_sil, n + 1)
                pool.wait_ge(p_top, n + 1)
                link(nc.gpsimd.tensor_tensor(rec[:, :, :], rec[:, :, :], sil[:, :, :], ALU.mult))
                nc.gpsimd.tensor_tensor(rec[:, :, :], rec[:, :, :], rest[:, :, :], ALU.mult).then_inc(p_w, 1)

            def normed_weights(n):
                pool.wait_ge(p_inv, n + 1)
                inv = wsum[:, 1, :].unsqueeze(2).to_broadcast([P, TPC, E])
                link(nc.gpsimd.tensor_tensor(cw2[:, :, 0:E].bitcast(F32R), rec[:, :, :], inv, ALU.mult))
                link(nc.gpsimd.tensor_tensor(rec[:, :, :], rec[:, :, :], inv, ALU.mult))
                nc.gpsimd.tensor_tensor(cw2[:, :, E:2 * E], rec[:, :, :], cw2[:, :, 0:E], ALU.subtract).then_inc(p_cw, 1)

            link(nc.gpsimd.memset(ident[:, :], 0.0))
            nc.gpsimd.affine_select(out=ident[:, :], in_=ident[:, :], compare_op=ALU.not_equal, fill=1.0,
                                    base=0, pattern=[[-1, P]], channel_multiplier=1).then_inc(s_id, 1)
            link(nc.gpsimd.memset(mhalf[:, :], -0.5))
            for f in range(2):
                for c in range(NCH):
                    n = f * NCH + c
                    if c == 0:
                        rstd(0, n, p_st, p_rs)
                        if f == 0:
                            for k in range(PRE):
                                piece_lo(k)
                        else:
                            weights(n)
                            normed_weights(n)
                    for u in range(UNITS):
                        if on_pool(u):
                            low_part(nc.gpsimd, n * UNITS + u).then_inc(s_glop, 1)
                        if n == 0 and u % 2 == 0 and PRE + u // 2 < 2 * WP:
                            piece_lo(PRE + u // 2)
                        if c + 1 < NCH:
                            if u == 4:
                                rstd(0, n + 1, p_st, p_rs)
                            if u == 22:
                                weights(n + 1)
                            if u == 25:
                                normed_weights(n + 1)
                        if f == 0 and c and u == 14:
                            rstd(1, c - 1, e_st, e_rs)
                if f == 0:
                    rstd(1, NCH - 1, e_st, e_rs)

        @block.scalar
        def _(act):
            def silu_unit(u, n):
                U = n * UNITS + u
                m = P if u else F
                act.wait_ge(s_hid, U + 1)
                if U >= NS:
                    act.wait_ge(s_gated, U - NS + 1)
                nc.scalar.activation(silu[0:m, U % NS, :], hid[U % 2][0:m, :], ACT.Silu).then_inc(s_silu, 1)

            def hi_unit(u, n):
                U = n * UNITS + u
                m = P if u else F
                act.wait_ge(s_gated, U + 1)
                if U >= NGP:
                    act.wait_ge(s_down, U - NGP + 1)
                nc.scalar.copy(gpart[0][0:m, U % NGP, :], gated[0:m, U % NG, :]).then_inc(s_ghi, 1)

            def pro_hi(n):
                act.wait_ge(p_xT, n + 1)
                nc.scalar.copy(xnT[n // NCH][0][:, n % 2, :], mp[:, :]).then_inc(p_hi, 1)

            def pro_sil(n):
                act.wait_ge(p_affs, n + 1)
                nc.scalar.activation(sil[:, :, :], aff[n // NCH][:, :, :], ACT.Silu).then_inc(p_sil, 1)

            def pro_cwT(n):
                act.wait_ge(p_cwT, n + 1)
                nc.scalar.copy(cwT[n // NCH][n % 2][:, :], mp[:, :]).then_inc(p_cwr, 1)

            def epi_y(n):
                act.wait_ge(s_down, (n + 1) * UNITS)
                if n:
                    act.wait_ge(e_yT, n)
                nc.scalar.mul(yT[:, :], yacc[n % 2][:, :], 0.5).then_inc(e_y, 1)

            def epi_hi(c):
                act.wait_ge(e_xT, c + 1)
                nc.scalar.copy(x2T[0][:, :], mq[:, :]).then_inc(e_hi, 1)

            def epi_proj_hi(c, k):
                act.wait_ge(e_pr, 3 * c + k + 1)
                nc.scalar.copy(proj_parts(c, k)[0], proj_bank(c, k)).then_inc(e_prhi, 1)

            def piece_hi(k):
                act.wait_ge(s_raw[k % NR], 16 * (k // NR + 1))
                nc.scalar.copy(piece(k, 0), raw[:, k % NR, :]).then_inc(s_whi, 1)

            def make_sel(k):
                at = slice(k * E // SP, (k + 1) * E // SP)
                nc.scalar.copy(sel[:, at, :], spread[:, at].bitcast(F32).unsqueeze(2)
                               .to_broadcast([P, E // SP, F])).then_inc(s_sel, 1)

            act.wait_ge(s_small, 16 * 6)
            nc.scalar.copy(small[0][:, :], raws[:, :]).then_inc(s_wh, 1)
            nc.scalar.copy(wsdn[0][:, :], rawd[:, :]).then_inc(s_wh, 1)
            act.wait_ge(s_spread, 1)
            make_sel(0)
            for f in range(2):
                for c in range(NCH):
                    n = f * NCH + c
                    if c == 0:
                        if f == 0:
                            piece_hi(0)
                            pro_hi(n)
                            for k in range(1, 6):
                                piece_hi(k)
                            pro_sil(n)
                            for k in range(6, PRE):
                                piece_hi(k)
                            for u in range(LEAD):
                                silu_unit(u, n)
                            for k in range(1, SP):
                                make_sel(k)
                            pro_cwT(n)
                    for u in range(UNITS):
                        if n or u >= LEAD:
                            silu_unit(u, n)
                        if n == 0 and u % 2 == 0 and PRE + u // 2 < 2 * WP:
                            piece_hi(PRE + u // 2)
                        if u or c:
                            hi_unit(*((u - 1, n) if u else (UNITS - 1, n - 1)))
                        if c + 1 < NCH:
                            if u == 12:
                                pro_hi(n + 1)
                            if u == 18:
                                pro_sil(n + 1)
                            if u == 31:
                                pro_cwT(n + 1)
                        if c:
                            if u == 5:
                                epi_y(n - 1)
                            if f == 0 and u == 19:
                                epi_hi(c - 1)
                            if f == 0 and u in (23, 26, 29)[:1 if c == NCH - 1 else 3]:
                                epi_proj_hi(c - 1, (23, 26, 29).index(u))
                    if c == NCH - 1:
                        hi_unit(UNITS - 1, n)
                        if f == 0:
                            epi_proj_hi(c - 1, 1)
                        epi_y(n)
                        if f == 0:
                            epi_proj_hi(c - 1, 2)
                            epi_hi(c)
                            for k in range(3):
                                epi_proj_hi(c, k)
                if f == 0:
                    def exp_bank(t, j):
                        if j == 0:
                            act.wait_ge(a_mx, t + 1)
                        if t:
                            act.wait_ge(a_t, KB * (t - 1) + j + 1)
                        nc.scalar.activation(prow[:, j * CH:(j + 1) * CH], lrow[:, j * CH:(j + 1) * CH], ACT.Exp,
                                             bias=nmax[:, t % 2:t % 2 + 1], accum_out=psums[:, t, j:j + 1]).then_inc(a_exp, 1)

                    def turn_hi(t, q):
                        act.wait_ge(a_t, 4 * t + q + 1)
                        if t // GT >= 2 and t % GT == 0 and q == 0:
                            act.wait_ge(a_o, t // GT - 1)
                        nc.scalar.copy(pT[0][:, t // GT % 2, 4 * q:4 * q + 4, t % GT * P:(t % GT + 1) * P],
                                       tb[q % 2][:, :].rearrange("p (k n) -> p k n", n=P)).then_inc(a_thi, 1)

                    def o_copy(g):
                        act.wait_ge(a_o, g + 1)
                        if g:
                            act.wait_ge(a_oT, g)
                        nc.scalar.copy(oT[:, :], ob[g % 2][:, 0:GW]).then_inc(a_oc, 1)

                    for t in range(NT):
                        if t == T_XT:
                            pro_hi(NCH)
                        exp_bank(t, 0)
                        exp_bank(t, 1)
                        turn_hi(t, 0)
                        exp_bank(t, 2)
                        turn_hi(t, 1)
                        exp_bank(t, 3)
                        turn_hi(t, 2)
                        turn_hi(t, 3)
                        if t % GT == 0 and t // GT >= 2:
                            o_copy(t // GT - 2)
                    pro_sil(NCH)
                    o_copy(NQ - 2)
                    for k in range(SP):
                        make_sel(k)
                    pro_cwT(NCH)
                    o_copy(NQ - 1)

        @block.vector
        def _(dve):
            steps = [0]

            def link(ins):
                steps[0] += 1
                ins.then_inc(s_dve, 1)
                dve.wait_ge(s_dve, steps[0])

            def gate_unit(u, n):
                U = n * UNITS + u
                dve.wait_ge(s_silu, U + 1)
                if U >= NG:
                    dve.wait_ge(s_ghi, U - NG + 1)
                    wait_low(dve, U - NG)
                if u == 0:
                    nc.vector.tensor_copy(gated[0:F, U % NG, :], silu[0:F, U % NS, :]).then_inc(s_gated, 1)
                    return
                R = n * PAIRS + u - 1
                dve.wait_ge(s_gate, R + 1)
                nc.vector.tensor_tensor(gated[:, U % NG, :], silu[:, U % NS, :], gate[R % 2], ALU.mult).then_inc(s_gated, 1)

            def lo_unit(u, n):
                if not on_pool(u):
                    low_part(nc.vector, n * UNITS + u).then_inc(s_glo, 1)

            def raw_stats(k, c, tiles):
                for i in tiles:
                    ins = nc.vector.bn_stats(stat[:, k, i, :], x[:, c * TPC + i, :])
                return ins

            def stats(k, c, done, tiles=range(TPC)):
                link(raw_stats(k, c, tiles))
                for i in range(TPC):
                    ins = nc.vector.bn_aggr(mv[:, k, i, :], stat[:, k, i, :])
                ins.then_inc(done, 1)

            def normed(k, n, c, dst, ready, done, tiles=range(TPC)):
                dve.wait_ge(ready, n + 1)
                for i in tiles:
                    ins = nc.vector.tensor_scalar(dst[:, i, :], x[:, c * TPC + i, :], mv[:, k, i, 0:1],
                                                  rs[:, k, 3, i:i + 1], ALU.subtract, ALU.mult)
                if TPC - 1 in tiles:
                    ins.then_inc(done, 1)

            def pro_lo(n):
                dve.wait_ge(p_hi, n + 1)
                hi, lo = (a[:, n % 2, :] for a in xnT[n // NCH])
                nc.vector.tensor_tensor(lo, mp[:, :], hi.bitcast(F32), ALU.subtract).then_inc(p_lo, 1)

            def bc(ap):
                return ap.unsqueeze(1).to_broadcast([P, TPC, E])

            def pro_aff(n, step):
                f = n // NCH
                ps = mp[:, 0:TPC * E].rearrange("p (t e) -> p t e", e=E)
                if step == 0:
                    dve.wait_ge(p_aff, n + 1)
                    link(nc.vector.tensor_scalar(rec[:, :, :], ps, 0.0, 2 * TINY, ALU.is_ge, ALU.mult))
                    nc.vector.scalar_tensor_tensor(out=aff[f][:, :, :], in0=ps, scalar=TINY, in1=rec[:, :, :],
                                                   op0=ALU.subtract, op1=ALU.add).then_inc(p_affs, 1)
                else:
                    nc.vector.tensor_tensor(biased[f][:, :, :], ps, bc(bias[:, :]), ALU.add).then_inc(p_bias, 1)

            def pro_top(n, step):
                b = biased[n // NCH]
                if step == 0:
                    dve.wait_ge(p_bias, n + 1)
                    for i in range(TPC):
                        ins = nc.vector.max(top[:, i, :], b[:, i, :])
                    ins.then_inc(p_max, 1)
                if step == 1:
                    dve.wait_ge(p_max, n + 1)
                    for i in range(TPC):
                        ins = nc.vector.match_replace(rest[:, i, :], top[:, i, :], b[:, i, :], LOWEST)
                    link(ins)
                    nc.vector.tensor_tensor(rest[:, :, :], rest[:, :, :], b[:, :, :], ALU.not_equal)
                if step == 2:
                    nc.vector.reciprocal(rec[:, :, :], aff[n // NCH][:, :, :]).then_inc(p_top, 1)

            def first_weights(n):
                for step in range(3):
                    pro_top(n, step)
                dve.wait_ge(p_sil, n + 1)
                dve.wait_ge(p_top, n + 1)
                link(nc.vector.tensor_tensor(rec[:, :, :], rec[:, :, :], sil[:, :, :], ALU.mult))
                nc.vector.tensor_tensor(rec[:, :, :], rec[:, :, :], rest[:, :, :], ALU.mult).then_inc(p_w, 1)
                pro_sum(n)
                dve.wait_ge(p_inv, n + 1)
                inv = wsum[:, 1, :].unsqueeze(2).to_broadcast([P, TPC, E])
                link(nc.vector.tensor_tensor(cw2[:, :, 0:E].bitcast(F32R), rec[:, :, :], inv, ALU.mult))
                link(nc.vector.tensor_tensor(rec[:, :, :], rec[:, :, :], inv, ALU.mult))
                nc.vector.tensor_tensor(cw2[:, :, E:2 * E], rec[:, :, :], cw2[:, :, 0:E], ALU.subtract).then_inc(p_cw, 1)

            def pro_sum(n):
                dve.wait_ge(p_w, n + 1)
                link(nc.vector.tensor_reduce(wsum[:, 0, :], rec[:, :, :], AX, ALU.add))
                link(nc.vector.tensor_scalar(wsum[:, 0, :], wsum[:, 0, :], 1e-8, None, ALU.add))
                nc.vector.reciprocal(wsum[:, 1, :], wsum[:, 0, :]).then_inc(p_inv, 1)

            def epi_x(n, c):
                dve.wait_ge(e_yT, n + 1)
                nc.vector.tensor_tensor(x[:, c * TPC:(c + 1) * TPC, :], x[:, c * TPC:(c + 1) * TPC, :],
                                        mq[:, :].rearrange("p (t d) -> p t d", d=D), ALU.add).then_inc(e_x, 1)

            def epi_lo(c):
                dve.wait_ge(e_hi, c + 1)
                nc.vector.tensor_tensor(x2T[1][:, :], mq[:, :], x2T[0][:, :].bitcast(F32), ALU.subtract).then_inc(e_lo, 1)

            def epi_proj_lo(c, k):
                dve.wait_ge(e_prhi, 3 * c + k + 1)
                dst = proj_parts(c, k)
                nc.vector.tensor_tensor(dst[1], proj_bank(c, k), dst[0].bitcast(F32), ALU.subtract).then_inc(e_prlo, 1)

            def epi_stats(c):
                dve.wait_ge(e_x, c + 1)
                stats(1, c, e_st)

            def max_bank(t, j):
                dve.wait_ge(a_l, KB * t + j + 1)
                return nc.vector.reduce_max(pmax[:, j:j + 1], lrow[:, j * CH:(j + 1) * CH], AX)

            def row_max(t):
                if t >= 2:
                    dve.wait_ge(a_exp, KB * (t - 1))
                nc.vector.tensor_reduce(nmax[:, t % 2:t % 2 + 1], pmax[:, :], AX, ALU.max, negate=True).then_inc(a_mx, 1)

            dve.wait_ge(s_x[0], 16)
            stats(0, 0, p_st)
            dve.wait_ge(s_id, 1)
            nc.vector.tensor_tensor(spread[:, :], ident[:, 0:E], ident[:, E:2 * E], ALU.add).then_inc(s_spread, 1)
            dve.wait_ge(s_wh, 2)
            nc.vector.tensor_tensor(small[1][:, :], raws[:, :], small[0][:, :].bitcast(F32), ALU.subtract).then_inc(s_wl, 1)
            nc.vector.tensor_tensor(wsdn[1][:, :], rawd[:, :], wsdn[0][:, :].bitcast(F32), ALU.subtract).then_inc(s_wl, 1)
            dve.wait_ge(s_bias, 16)
            for f in range(2):
                for c in range(NCH):
                    n = f * NCH + c
                    if c == 0:
                        if f == 0:
                            normed(0, n, 0, xn[f], p_rs, p_xn)
                            pro_lo(n)
                            pro_aff(n, 0)
                            pro_aff(n, 1)
                            first_weights(n)
                    for u in range(UNITS):
                        gate_unit(u, n)
                        if u or c:
                            lo_unit(*((u - 1, n) if u else (UNITS - 1, n - 1)))
                        if c + 1 < NCH:
                            if u == 0:
                                if f == 0:
                                    dve.wait_ge(s_x[c + 1], 16)
                                raw_stats(0, c + 1, (0, 1))
                            if u == 2:
                                stats(0, c + 1, p_st, (2, 3))
                            if u == 6:
                                normed(0, n + 1, c + 1, xn[f], p_rs, p_xn, (0, 1))
                            if u == 8:
                                normed(0, n + 1, c + 1, xn[f], p_rs, p_xn, (2, 3))
                            if u == 12:
                                pro_lo(n + 1)
                            if u == 15:
                                pro_aff(n + 1, 0)
                            if u == 16:
                                pro_aff(n + 1, 1)
                            if u == 18:
                                pro_top(n + 1, 0)
                            if u == 20:
                                pro_top(n + 1, 1)
                            if u == 22:
                                pro_top(n + 1, 2)
                            if u == 24:
                                pro_sum(n + 1)
                        if c:
                            if u == 9:
                                epi_x(n - 1, c - 1)
                            if f == 0:
                                if u == 10:
                                    epi_stats(c - 1)
                                if u == 16:
                                    normed(1, c - 1, c - 1, xn2, e_rs, e_xn, (0, 1))
                                if u == 17:
                                    normed(1, c - 1, c - 1, xn2, e_rs, e_xn, (2, 3))
                                if u == 19:
                                    epi_lo(c - 1)
                                if u in (23, 26, 29)[:1 if c == NCH - 1 else 3]:
                                    epi_proj_lo(c - 1, (23, 26, 29).index(u))
                    if c == NCH - 1:
                        lo_unit(UNITS - 1, n)
                        if f == 0:
                            epi_proj_lo(c - 1, 1)
                        epi_x(n, c)
                        if f == 0:
                            epi_stats(c)
                            for j in range(KB - 1):
                                max_bank(0, j)
                            epi_proj_lo(c - 1, 2)
                            normed(1, c, c, xn2, e_rs, e_xn)
                            epi_lo(c)
                            epi_proj_lo(c, 0)
                            epi_proj_lo(c, 1)
                            link(max_bank(0, KB - 1))
                            row_max(0)
                            epi_proj_lo(c, 2)
                if f == 0:
                    def turn_lo(t, q):
                        dve.wait_ge(a_thi, 4 * t + q + 1)
                        at = (slice(None), t // GT % 2, slice(4 * q, 4 * q + 4), slice(t % GT * P, (t % GT + 1) * P))
                        nc.vector.tensor_tensor(pT[1][at], tb[q % 2][:, :].rearrange("p (k n) -> p k n", n=P),
                                                pT[0][at].bitcast(F32), ALU.subtract).then_inc(a_tlo, 1)

                    def inverse(g):
                        link(nc.vector.tensor_reduce(pinv[:, g % 2, :, 0], psums[:, GT * g:GT * (g + 1), :], AX, ALU.add))
                        link(nc.vector.reciprocal(pinv[:, g % 2, :, 1], pinv[:, g % 2, :, 0]))
                        link(nc.vector.tensor_scalar(pinv[:, g % 2, :, 0], pinv[:, g % 2, :, 1], NORM, None, ALU.mult))

                    def add_o(g):
                        dve.wait_ge(a_oT, g + 1)
                        inverse(g)
                        for i in range(GT):
                            ins = nc.vector.scalar_tensor_tensor(
                                out=x[:, GT * g + i, :], in0=ob[g % 2][:, GW + i * P:GW + (i + 1) * P],
                                scalar=pinv[:, g % 2, i, 0:1], in1=x[:, GT * g + i, :], op0=ALU.mult, op1=ALU.add)
                        ins.then_inc(a_x, 1)

                    for t in range(NT):
                        if t == T_XT:
                            normed(0, NCH, 0, xn[1], p_rs, p_xn)
                        for j in range(KB):
                            if t:
                                turn_lo(t - 1, j)
                                ins = max_bank(t, j)
                        if t:
                            link(ins)
                            row_max(t)
                        if t % GT == 1 and t // GT >= 2:
                            add_o(t // GT - 2)
                        if t == T_XT - 1:
                            stats(0, 0, p_st)
                        if t == T_XT:
                            pro_lo(NCH)
                        if t == T_AFF:
                            pro_aff(NCH, 0)
                            pro_aff(NCH, 1)
                            pro_top(NCH, 0)
                    pro_top(NCH, 1)
                    pro_top(NCH, 2)
                    for j in range(KB):
                        turn_lo(NT - 1, j)
                    pro_sum(NCH)
                    add_o(NQ - 2)
                    add_o(NQ - 1)
                    dve.wait_ge(a_x, NQ)

        @block.tensor
        def _(pe):
            def product(out, a, b):
                nc.tensor.matmul(out, a[0], b[1], start=True, stop=False)
                nc.tensor.matmul(out, a[1], b[0], start=False, stop=False)
                return nc.tensor.matmul(out, a[0], b[0], start=False, stop=True)

            def up(u, n):
                U = n * UNITS + u
                if n == 0 and u and (u - 1) % (PAIRS // WP) == 0:
                    pe.wait_ge(s_w, 2 * ((u - 1) // (PAIRS // WP)) + 1)
                if U >= 2:
                    pe.wait_ge(s_silu, U - 1)
                w = [a[:, (u - 1) * P:u * P] for a in wup] if u else wsup
                product(hid[U % 2][0:P if u else F, :], w, [a[:, n % 2, :] for a in xnT[n // NCH]]).then_inc(s_hid, 1)

            def spread_gate(u, n):
                if u:
                    R = n * PAIRS + u - 1
                    if R >= 2:
                        pe.wait_ge(s_gated, n * UNITS + u - 1 if u > 2 else n * UNITS + u - 2)
                    if n % NCH == 0 and (u - 1) % (PAIRS // SP) == 0:
                        pe.wait_ge(s_sel, n // NCH * SP + (u - 1) // (PAIRS // SP) + 1)
                    one = sel[:, 2 * u - 2:2 * u, :].rearrange("p e f -> p (e f)")
                    nc.tensor.matmul(gate[R % 2], one, cwT[n // NCH][n % 2][:, :], start=True, stop=True).then_inc(s_gate, 1)

            def down(u, n):
                U = n * UNITS + u
                m = P if u else F
                if n == 0 and u and (u - 1) % (PAIRS // WP) == 0:
                    pe.wait_ge(s_w, 2 * ((u - 1) // (PAIRS // WP)) + 2)
                if u == 0 and n % NCH >= 2:
                    pe.wait_ge(e_y, n - 1)
                wait_low(pe, U)
                w = [a[:, u - 1, :] for a in wdn] if u else [a[:, :] for a in wsdn]
                g = [a[0:m, U % NGP, :] for a in gpart]
                y = yacc[n % 2][:, :]
                nc.tensor.matmul(y, w[0], g[1], start=(u == 0), stop=False)
                nc.tensor.matmul(y, w[1], g[0], start=False, stop=False)
                nc.tensor.matmul(y, w[0], g[0], start=False, stop=(u == UNITS - 1)).then_inc(s_down, 1)

            def turn(src, ps, done):
                for i in range(TPC):
                    ins = nc.tensor.transpose(ps[:, i * P:(i + 1) * P], src[:, i * P:(i + 1) * P], ident[:, :])
                ins.then_inc(done, 1)

            def pro_xT(n):
                pe.wait_ge(p_xn, n + 1)
                if n:
                    pe.wait_ge(p_cwr, n)
                turn(flat(xn[n // NCH]), mp, p_xT)

            def pro_aff(n):
                pe.wait_ge(p_lo, n + 1)
                for i in range(TPC):
                    ins = product(mp[:, i * E:(i + 1) * E], [a[:, n % 2, i * P:(i + 1) * P] for a in xnT[n // NCH]], cen)
                ins.then_inc(p_aff, 1)

            def pro_cw(n):
                pe.wait_ge(p_cw, n + 1)
                turn(flat(cw2), mp, p_cwT)

            def epi_yT(n):
                pe.wait_ge(e_y, n + 1)
                if 0 < n <= NCH:
                    pe.wait_ge(e_prlo, 3 * n - 2 if n == NCH - 1 else 3 * n)
                elif n:
                    pe.wait_ge(e_x, n)
                turn(yT, mq, e_yT)

            def epi_xT(c):
                pe.wait_ge(e_xn, c + 1)
                turn(flat(xn2), mq, e_xT)

            def epi_proj(c, k):
                if k == 0:
                    pe.wait_ge(e_lo, c + 1)
                elif c < NCH - 2:
                    pe.wait_ge(e_prlo, 3 * c + k)
                out = proj_bank(c, k)
                if k < 2:
                    ins = product(out, (wk, wq)[k], [a[:, :] for a in x2T])
                else:
                    for i in range(TPC):
                        ins = product(out[:, i * D:(i + 1) * D], [a[:, i * P:(i + 1) * P] for a in x2T], wv)
                ins.then_inc(e_pr, 1)

            def logits(t, j):
                if t:
                    pe.wait_ge(a_exp, KB * (t - 1) + j + 1)
                product(lrow[:, j * CH:(j + 1) * CH], [a[:, t * P:(t + 1) * P] for a in qT],
                        [a[:, j * CH:(j + 1) * CH] for a in kT]).then_inc(a_l, 1)

            pe.wait_ge(s_id, 1)
            for f in range(2):
                for c in range(NCH):
                    n = f * NCH + c
                    if n == 0:
                        pro_xT(n)
                        pe.wait_ge(s_wl, 2)
                        pro_aff(n)
                        for u in range(LEAD):
                            up(u, n)
                        pro_cw(n)
                    pe.wait_ge(p_cwr, n + 1)
                    for u in range(UNITS):
                        if n or u >= LEAD:
                            up(u, n)
                        spread_gate(u, n)
                        if u >= LAG:
                            down(u - LAG, n)
                        elif c:
                            down(UNITS - LAG + u, n - 1)
                        if c + 1 < NCH:
                            if u == 11:
                                pro_xT(n + 1)
                            if u == 14:
                                pro_aff(n + 1)
                            if u == 30:
                                pro_cw(n + 1)
                        if c:
                            if u == 8:
                                epi_yT(n - 1)
                            if f == 0:
                                if u == 18:
                                    epi_xT(c - 1)
                                if u in (22, 25, 28)[:1 if c == NCH - 1 else 3]:
                                    epi_proj(c - 1, (22, 25, 28).index(u))
                    if c == NCH - 1:
                        for u in range(UNITS - LAG, UNITS):
                            down(u, n)
                            if f == 0 and u == UNITS - LAG:
                                epi_proj(c - 1, 1)
                        if f == 0:
                            pe.wait_ge(e_prlo, 3 * c - 2)
                            logits(0, 0)
                            logits(0, 1)
                        epi_yT(n)
                        if f == 0:
                            logits(0, 2)
                            epi_proj(c - 1, 2)
                            epi_xT(c)
                            for k in range(3):
                                epi_proj(c, k)
                            pe.wait_ge(e_prlo, 3 * c + 1)
                            logits(0, KB - 1)
                if f == 0:
                    def turn_p(t, q):
                        pe.wait_ge(a_exp, KB * t + q + 1)
                        if 4 * t + q >= 2:
                            pe.wait_ge(a_tlo, 4 * t + q - 1)
                        if q == 0 and t == T_XT:
                            pe.wait_ge(p_lo, NCH + 1)
                        if q == 0 and t == T_AFF:
                            pe.wait_ge(p_bias, NCH + 1)
                        turn(prow[:, q * CH:(q + 1) * CH], tb[q % 2], a_t)

                    def weigh(g, ks):
                        for k in ks:
                            if k == 0 and g >= 2:
                                pe.wait_ge(a_x, g - 1)
                            if k % 4 == 0:
                                pe.wait_ge(a_tlo, 4 * (GT * g + GT - 1) + k // 4 + 1)
                            p = [a[:, g % 2, k, :] for a in pT]
                            o = ob[g % 2][:, 0:GW]
                            nc.tensor.matmul(o, v[0][:, k, :], p[1], start=(k == 0), stop=False)
                            nc.tensor.matmul(o, v[1][:, k, :], p[0], start=False, stop=False)
                            ins = nc.tensor.matmul(o, v[0][:, k, :], p[0], start=False, stop=(k == NT - 1))
                            if k == NT - 1:
                                ins.then_inc(a_o, 1)

                    def turn_o(g):
                        pe.wait_ge(a_oc, g + 1)
                        for i in range(GT):
                            ins = nc.tensor.transpose(ob[g % 2][:, GW + i * P:GW + (i + 1) * P],
                                                      oT[:, i * P:(i + 1) * P], ident[:, :])
                        ins.then_inc(a_oT, 1)

                    pe.wait_ge(e_prlo, 3 * NCH)
                    half = NT // GT
                    for t in range(NT):
                        g = t // GT
                        at = t % GT * half
                        for j, n_k in enumerate(SHARE):
                            if t:
                                turn_p(t - 1, j)
                                logits(t, j)
                            if j == KB - 1:
                                if t % GT == 1 and g >= 2:
                                    turn_o(g - 2)
                                if t == T_XT:
                                    pe.wait_ge(a_tlo, 4 * (t - 1) + 3)
                                    pro_xT(NCH)
                                if t == T_AFF:
                                    pe.wait_ge(a_tlo, 4 * (t - 1) + 3)
                                    pro_aff(NCH)
                            if g:
                                weigh(g - 1, range(at, at + n_k))
                                at += n_k
                    for j in range(KB):
                        turn_p(NT - 1, j)
                    weigh(NQ - 1, range(NT))
                    turn_o(NQ - 2)
                    pro_cw(NCH)
                    turn_o(NQ - 1)


def kernel(L0_attn_x, L0_attn_Wq, L0_attn_Wk, L0_attn_Wv, L0_ffn_centroids, L0_ffn_expert_biases,
           L0_ffn_Ws_up, L0_ffn_Ws_down, L0_ffn_W_up, L0_ffn_W_down):
    import numpy as np
    import concourse.bacc as bacc
    from concourse.bass_utils import run_bass_kernel_spmd as run

    x = np.asarray(L0_attn_x)
    b, s, d = x.shape
    w_up, w_down = np.asarray(L0_ffn_W_up), np.asarray(L0_ffn_W_down)
    e, _, f = w_up.shape
    arrays = {
        "x": x.reshape(b * s, d),
        "w_up": w_up.transpose(1, 0, 2).reshape(d, e * f),
        "w_down": w_down.reshape(e // 2, 2 * f, d).transpose(1, 0, 2).reshape(2 * f, e // 2 * d),
        "ws_up": np.asarray(L0_ffn_Ws_up),
        "ws_down": np.asarray(L0_ffn_Ws_down),
        "centroids": np.asarray(L0_ffn_centroids).T,
        "biases": np.asarray(L0_ffn_expert_biases),
        "wq": np.asarray(L0_attn_Wq).T,
        "wk": np.asarray(L0_attn_Wk).T,
        "wv": np.asarray(L0_attn_Wv).T,
    }
    arrays = {n: np.ascontiguousarray(a) for n, a in arrays.items()}
    nc = bacc.Bacc("TRN2", target_bir_lowering=False, num_devices=1)
    args = [nc.dram_tensor("in_" + n, a.shape, mybir.dt.from_np(a.dtype), kind="ExternalInput").ap() for n, a in arrays.items()]
    out = nc.dram_tensor("out_dram", (b * s, d), F32, kind="ExternalOutput").ap()
    macaron_kernel(nc, *args, out)
    r = run(nc, [{"in_" + n: a for n, a in arrays.items()}], core_ids=[0])
    return r.results[0]["out_dram"].reshape(b, s, d)
```

```python
from contextlib import ExitStack

import concourse.bass as bass
from concourse import mybir

F32 = mybir.dt.float32
F32R = mybir.dt.float32r
ALU = mybir.AluOpType
ACT = mybir.ActivationFunctionType
AX = mybir.AxisListType.X

P = 128
CH = 512
TPC = CH // P
EPS = 1e-5
TOP = 8
LAG = 4
NS, NG, NGP = 3, 3, 5
NB = 5
FIRST_DMA = 5
GAP, EVERY = 12, 8
GT = 2
PRE = 8
LEAD = 2
T_XT, T_AFF = 12, 13
SHARE = (0, 0, 1, 7)
LOWEST = -3.4e38
TINY = 1e-15


def macaron_kernel(nc, x_d, wup_d, wdn_d, wsup_d, wsdn_d, cent_d, bias_d, wq_d, wk_d, wv_d, gates_d, out_d):
    T, D = x_d.shape
    E = cent_d.shape[1]
    F = wsup_d.shape[1]
    assert D == P and 2 * F == P and 2 * E == P and T % CH == 0
    NT = T // P
    NCH = T // CH
    PAIRS = E // 2
    UNITS = PAIRS + 1
    NQ = NT // GT
    GW = GT * P
    KB = T // CH
    NORM = 1.0 / float(D) ** 0.5
    NR = 4
    WP = 8
    PW = E * F // WP
    BY_PE = list(range(1, FIRST_DMA)) + list(range(FIRST_DMA + GAP, UNITS, EVERY))
    BY_DMA = [u for u in range(1, UNITS) if u not in BY_PE]
    ND, NP = len(BY_DMA), len(BY_PE)
    SP = 2

    x_v = x_d.rearrange("(t p) d -> p t d", p=P)
    out_v = out_d.rearrange("(t p) d -> p t d", p=P)

    with ExitStack() as ctx:
        def sb(name, shape, dt=F32, stack=ctx):
            return stack.enter_context(nc.sbuf_tensor(name, shape, dt))

        def sem(name):
            return ctx.enter_context(nc.semaphore(name))

        x = sb("x", [P, NT, D])
        ident = sb("ident", [P, P])
        spread = sb("spread", [P, E], F32R)
        wup = [sb("wup_hi", [P, E * F], F32R), sb("wup_lo", [P, E * F], F32R)]
        wdn = [sb("wdn_hi", [P, PAIRS, D], F32R), sb("wdn_lo", [P, PAIRS, D], F32R)]
        early = ctx.enter_context(ExitStack())
        xnT_b = [sb("xnT_hi_b", [P, 2, CH], F32R, early)]
        xn_b, cwT_b1 = sb("xn_b", [P, TPC, D], F32, early), sb("cwT_b1", [P, CH], F32R, early)
        xnT_b.append(sb("xnT_lo_b", [P, 2, CH], F32R, early))
        biased_b, aff_b = sb("biased_b", [P, TPC, E], F32, early), sb("aff_b", [P, TPC, E], F32, early)
        early.close()
        qT = [sb("qT_hi", [P, T], F32R), sb("qT_lo", [P, T], F32R)]
        kT = [sb("kT_hi", [P, T], F32R), sb("kT_lo", [P, T], F32R)]
        v = [sb("v_hi", [P, NT, D], F32R), sb("v_lo", [P, NT, D], F32R)]
        SM = E + F + 3 * D
        small = [sb("small_hi", [P, SM], F32R), sb("small_lo", [P, SM], F32R)]
        wsdn = [sb("wsdn_hi", [F, D], F32R), sb("wsdn_lo", [F, D], F32R)]
        bias = sb("bias", [P, E])
        mhalf = sb("mhalf", [P, TPC])
        cen = [s[:, 0:E] for s in small]
        wsup = [s[:, E:E + F] for s in small]
        wq, wk, wv = ([s[:, E + F + i * D:E + F + (i + 1) * D] for s in small] for i in range(3))

        cwT_0 = sb("cwT_0", [P, CH], F32R)
        stat = sb("stat", [P, 2, TPC, 6])
        mv = sb("mv", [P, 2, TPC, 2])
        rs = sb("rs", [P, 2, 4, TPC])
        rec = sb("rec", [P, TPC, E])
        sil = sb("sil", [P, TPC, E])
        rest = sb("rest", [P, TPC, E])
        top = sb("top", [P, TPC, TOP])
        wsum = sb("wsum", [P, 2, TPC])
        cw2 = sb("cw2", [P, TPC, 2 * E])

        ffn = ctx.enter_context(ExitStack())
        sel = sb("sel", [P, NP, 2, F], F32R, ffn)
        gates = sb("gates", [E, CH], F32, ffn)
        wide = sb("wide", [P, NB, CH], F32, ffn)
        xnT_a = [sb("xnT_hi_a", [P, 2, CH], F32R, ffn), sb("xnT_lo_a", [P, 2, CH], F32R, ffn)]
        xn_a, cwT_a1 = sb("xn_a", [P, TPC, D], F32, ffn), sb("cwT_a1", [P, CH], F32R, ffn)
        biased_a, aff_a = sb("biased_a", [P, TPC, E], F32, ffn), sb("aff_a", [P, TPC, E], F32, ffn)
        silu = sb("silu", [P, NS, CH], F32, ffn)
        gated = sb("gated", [P, NG, CH], F32, ffn)
        with ExitStack() as first:
            raw = sb("raw", [P, NR, PW], F32, first)
        x2T = [sb("x2T_hi", [P, CH], F32R, ffn), sb("x2T_lo", [P, CH], F32R, ffn)]
        yT = sb("yT", [P, CH], F32, ffn)
        xn2 = sb("xn2", [P, TPC, D], F32, ffn)
        with ExitStack() as first:
            raws = sb("raws", [P, SM], F32, first)
            rawd = sb("rawd", [F, D], F32, first)
        gpart = [sb("gpart_hi", [P, NGP, CH], F32R, ffn), sb("gpart_lo", [P, NGP, CH], F32R, ffn)]
        ffn.close()
        xnT, xn, cwT = [xnT_a, xnT_b], [xn_a, xn_b], [[cwT_0, cwT_a1], [cwT_0, cwT_b1]]
        biased, aff = [biased_a, biased_b], [aff_a, aff_b]
        pT = [sb("pT_hi", [P, 2, NT, GW], F32R), sb("pT_lo", [P, 2, NT, GW], F32R)]
        prow = sb("prow", [P, T])
        pmax = sb("pmax", [P, KB])
        nmax = sb("nmax", [P, 2])
        psums = sb("psums", [P, NT, KB])
        pinv = sb("pinv", [P, 2, GT, 2])
        oT = sb("oT", [P, GW])

        bank = [ctx.enter_context(nc.psum_tensor(f"bank{i}", [P, CH], F32)) for i in range(4)]
        lrow = ctx.enter_context(nc.psum_tensor("lrow", [P, 4 * CH], F32))
        hid = [lrow[:, 0:CH], lrow[:, CH:2 * CH]]
        gate = [lrow[:, 2 * CH:3 * CH], lrow[:, 3 * CH:4 * CH]]
        yacc = [bank[0], bank[1]]
        mp, mq = bank[2], bank[3]
        tb, ob = [bank[2], bank[3]], [bank[0], bank[1]]

        s_x = [sem(f"x_in{c}") for c in range(NCH)]
        s_small, s_bias = sem("small_in"), sem("bias_in")
        s_raw = [sem(f"raw_in{i}") for i in range(NR)]
        s_out = sem("out_stored")
        s_pool = sem("pool_step")
        s_id, s_spread = sem("ident_made"), sem("spread_made")
        s_wh, s_wl = sem("small_hi_made"), sem("small_lo_made")
        s_whi = sem("weight_piece_hi")
        s_w = sem("weight_piece_split")
        s_sel = sem("sel_piece_made")
        s_gates, s_gout = sem("gates_copied"), sem("gates_stored")
        s_wide = [sem(f"gates_spread{i}") for i in range(NB)]
        s_hid, s_gate = sem("hidden_ready"), sem("gate_ready")
        s_silu, s_gated = sem("silu_done"), sem("gated_done")
        s_ghi, s_glo, s_glop = sem("gated_hi_done"), sem("gated_lo_done_dve"), sem("gated_lo_done_pool")
        s_down = sem("down_done")
        s_dve = sem("dve_step")
        p_st, p_rs, p_xn, p_xT, p_hi, p_lo = (sem("p_" + n) for n in ("stats", "rstd", "xn", "xT", "hi", "lo"))
        p_aff, p_affs, p_bias, p_max, p_sil, p_top, p_w, p_inv, p_cw, p_cwT, p_cwr = (
            sem("p_" + n) for n in ("aff", "aff_read", "biased", "max", "sil", "top", "w", "inv", "cw", "cwT", "cwT_read"))
        e_y, e_yT, e_x, e_st, e_rs, e_xn, e_xT, e_hi, e_lo = (
            sem("e_" + n) for n in ("y", "yT", "x", "stats", "rstd", "xn", "xT", "hi", "lo"))
        e_pr, e_prhi, e_prlo = sem("e_proj"), sem("e_proj_hi"), sem("e_proj_lo")
        a_l, a_mx, a_exp, a_t, a_thi, a_tlo = (sem("a_" + n) for n in ("logits", "max", "exp", "pT", "pT_hi", "pT_lo"))
        a_o, a_oc, a_oT, a_x = (sem("a_" + n) for n in ("o", "o_copied", "oT", "x"))

        def proj_bank(c, k):
            if c == NCH - 1:
                return (lrow[:, (KB - 1) * CH:KB * CH], bank[0][:, :], bank[1][:, :])[k]
            return (mq, bank[0], mp)[k][:, :] if c == NCH - 2 else mq[:, :]

        def proj_parts(c, k):
            return [(kT[h][:, c * CH:(c + 1) * CH], qT[h][:, c * CH:(c + 1) * CH],
                     v[h][:, c * TPC:(c + 1) * TPC, :].rearrange("p t d -> p (t d)"))[k] for h in range(2)]

        def pe_unit(R):
            return R // NP * UNITS + BY_PE[R % NP]

        def dma_unit(G):
            return G // ND * UNITS + BY_DMA[G % ND]

        def on_pool(u):
            return u % 2 == 1

        def lows(U, pool):
            units = [u for u in range(UNITS) if on_pool(u) == pool]
            return U // UNITS * len(units) + sum(u <= U % UNITS for u in units)

        def wait_low(eng, U):
            pool = on_pool(U % UNITS)
            eng.wait_ge(s_glop if pool else s_glo, lows(U, pool))

        def flat(t):
            return t[:, :, :].rearrange("p t d -> p (t d)")

        def low_part(eng, U):
            m = P if U % UNITS else F
            eng.wait_ge(s_ghi, U + 1)
            return eng.tensor_tensor(gpart[1][0:m, U % NGP, :], gated[0:m, U % NG, :],
                                     gpart[0][0:m, U % NGP, :].bitcast(F32), ALU.subtract)

        def piece(k, part):
            w = (wup[part], flat(wdn[part]))[k % 2]
            return w[:, (k // 2) * PW:(k // 2 + 1) * PW]

        block = ctx.enter_context(nc.Block())

        @block.sync
        def _(sp):
            def load_x(c):
                sp.dma_start(x[:, c * TPC:(c + 1) * TPC, :], x_v[:, c * TPC:(c + 1) * TPC, :]).then_inc(s_x[c], 16)

            load_x(0)
            for src, lo, n in ((cent_d, 0, E), (wsup_d, E, F), (wq_d, E + F, D),
                               (wk_d, E + F + D, D), (wv_d, E + F + 2 * D, D)):
                sp.dma_start(raws[:, lo:lo + n], src).then_inc(s_small, 16)
            sp.dma_start(rawd[:, :], wsdn_d).then_inc(s_small, 16)
            sp.dma_start(bias[:, :], bias_d.partition_broadcast(P)).then_inc(s_bias, 16)
            def load_piece(k):
                if k >= NR:
                    sp.wait_ge(s_w, k - NR + 1)
                src = (wup_d, wdn_d)[k % 2][:, (k // 2) * PW:(k // 2 + 1) * PW]
                sp.dma_start(raw[:, k % NR, :], src).then_inc(s_raw[k % NR], 16)

            for k in range(PRE + NR):
                if NR <= k < NR + NCH - 1:
                    load_x(k - NR + 1)
                load_piece(k)
            for n in range(2 * NCH):
                sp.wait_ge(s_gates, n + 1)
                sp.dma_start(gates_d[n], gates[:, :]).then_inc(s_gout, 16)
                sp.wait_ge(s_gout, 16 * (n + 1))
                for i, u in enumerate(BY_DMA):
                    G = n * ND + i
                    if n == 0 and NB <= i < NB + 2 * WP - PRE - NR:
                        load_piece(PRE + NR + i - NB)
                    if G >= NB:
                        sp.wait_ge(s_gated, dma_unit(G - NB) + 1)
                    for e in range(2):
                        sp.dma_start(wide[e * F:(e + 1) * F, G % NB, :], gates_d[n, 2 * u - 2 + e, :].partition_broadcast(F)
                                     ).then_inc(s_wide[G % NB], 16)
            for c in range(NCH):
                sp.wait_ge(e_x, NCH + c + 1)
                sp.dma_start(out_v[:, c * TPC:(c + 1) * TPC, :], x[:, c * TPC:(c + 1) * TPC, :]).then_inc(s_out, 16)
            sp.wait_ge(s_out, 16 * NCH)

        @block.gpsimd
        def _(pool):
            steps = [0]

            def link(ins):
                steps[0] += 1
                ins.then_inc(s_pool, 1)
                pool.wait_ge(s_pool, steps[0])

            def rstd(k, n, stats, done):
                pool.wait_ge(stats, n + 1)
                ve, y = (rs[:, k, i, :] for i in range(2))
                link(nc.gpsimd.tensor_scalar(ve, mv[:, k, :, 1], EPS, None, ALU.add))
                nc.gpsimd.tensor_tensor(y, ve, mhalf[:, :], ALU.pow).then_inc(done, 1)

            def piece_lo(k):
                pool.wait_ge(s_whi, k + 1)
                nc.gpsimd.tensor_tensor(piece(k, 1), raw[:, k % NR, :], piece(k, 0).bitcast(F32), ALU.subtract).then_inc(s_w, 1)

            def weights(n):
                pool.wait_ge(p_sil, n + 1)
                pool.wait_ge(p_top, n + 1)
                link(nc.gpsimd.tensor_tensor(rec[:, :, :], rec[:, :, :], sil[:, :, :], ALU.mult))
                nc.gpsimd.tensor_tensor(rec[:, :, :], rec[:, :, :], rest[:, :, :], ALU.mult).then_inc(p_w, 1)

            def normed_weights(n):
                pool.wait_ge(p_inv, n + 1)
                inv = wsum[:, 1, :].unsqueeze(2).to_broadcast([P, TPC, E])
                nc.gpsimd.tensor_tensor(rest[:, :, :].bitcast(F32R), rec[:, :, :], inv, ALU.mult)
                link(nc.gpsimd.tensor_tensor(cw2[:, :, 0:E], rec[:, :, :], inv, ALU.mult))
                nc.gpsimd.tensor_tensor(cw2[:, :, E:2 * E], cw2[:, :, 0:E], rest[:, :, :], ALU.subtract).then_inc(p_cw, 1)

            link(nc.gpsimd.memset(ident[:, :], 0.0))
            nc.gpsimd.affine_select(out=ident[:, :], in_=ident[:, :], compare_op=ALU.not_equal, fill=1.0,
                                    base=0, pattern=[[-1, P]], channel_multiplier=1).then_inc(s_id, 1)
            link(nc.gpsimd.memset(mhalf[:, :], -0.5))
            for f in range(2):
                for c in range(NCH):
                    n = f * NCH + c
                    if c == 0:
                        rstd(0, n, p_st, p_rs)
                    if n == 0:
                        for k in range(PRE):
                            piece_lo(k)
                    for u in range(UNITS):
                        if on_pool(u):
                            low_part(nc.gpsimd, n * UNITS + u).then_inc(s_glop, 1)
                        if n == 0 and u % 2 == 0 and PRE + u // 2 < 2 * WP:
                            piece_lo(PRE + u // 2)
                        if c + 1 < NCH:
                            if u == 4:
                                rstd(0, n + 1, p_st, p_rs)
                            if u == 22:
                                weights(n + 1)
                            if u == 25:
                                normed_weights(n + 1)
                        if f == 0 and c and u == 14:
                            rstd(1, c - 1, e_st, e_rs)
                if f == 0:
                    rstd(1, NCH - 1, e_st, e_rs)

        @block.scalar
        def _(act):
            def silu_unit(u, n):
                U = n * UNITS + u
                m = P if u else F
                act.wait_ge(s_hid, U + 1)
                if U >= NS:
                    act.wait_ge(s_gated, U - NS + 1)
                nc.scalar.activation(silu[0:m, U % NS, :], hid[U % 2][0:m, :], ACT.Silu).then_inc(s_silu, 1)

            def hi_unit(u, n):
                U = n * UNITS + u
                m = P if u else F
                act.wait_ge(s_gated, U + 1)
                if U >= NGP:
                    act.wait_ge(s_down, U - NGP + 1)
                nc.scalar.copy(gpart[0][0:m, U % NGP, :], gated[0:m, U % NG, :]).then_inc(s_ghi, 1)

            def pro_hi(n):
                act.wait_ge(p_xT, n + 1)
                nc.scalar.copy(xnT[n // NCH][0][:, n % 2, :], mp[:, :]).then_inc(p_hi, 1)

            def pro_sil(n):
                act.wait_ge(p_affs, n + 1)
                nc.scalar.activation(sil[:, :, :], aff[n // NCH][:, :, :], ACT.Silu).then_inc(p_sil, 1)

            def pro_cwT(n):
                act.wait_ge(p_cwT, n + 1)
                nc.scalar.copy(cwT[n // NCH][n % 2][:, :], mp[:, :]).then_inc(p_cwr, 1)
                if n:
                    act.wait_ge(s_gout, 16 * n)
                nc.scalar.copy(gates[:, :], mp[0:E, :]).then_inc(s_gates, 1)

            def epi_y(n):
                act.wait_ge(s_down, (n + 1) * UNITS)
                if n:
                    act.wait_ge(e_yT, n)
                nc.scalar.mul(yT[:, :], yacc[n % 2][:, :], 0.5).then_inc(e_y, 1)

            def epi_hi(c):
                act.wait_ge(e_xT, c + 1)
                nc.scalar.copy(x2T[0][:, :], mq[:, :]).then_inc(e_hi, 1)

            def epi_proj_hi(c, k):
                act.wait_ge(e_pr, 3 * c + k + 1)
                nc.scalar.copy(proj_parts(c, k)[0], proj_bank(c, k)).then_inc(e_prhi, 1)

            def piece_hi(k):
                act.wait_ge(s_raw[k % NR], 16 * (k // NR + 1))
                nc.scalar.copy(piece(k, 0), raw[:, k % NR, :]).then_inc(s_whi, 1)

            def make_sel(k):
                run = FIRST_DMA - 1
                at, src = ((slice(0, run), slice(0, run)), (slice(run, NP), slice(BY_PE[run] - 1, PAIRS, EVERY)))[k]
                cols = spread[:, :].bitcast(F32).rearrange("p (i e) -> p i e", e=2)[:, src, :]
                nc.scalar.copy(sel[:, at, :, :], cols.unsqueeze(3).to_broadcast([P, at.stop - at.start, 2, F])).then_inc(s_sel, 1)

            act.wait_ge(s_small, 16 * 6)
            nc.scalar.copy(small[0][:, :], raws[:, :]).then_inc(s_wh, 1)
            nc.scalar.copy(wsdn[0][:, :], rawd[:, :]).then_inc(s_wh, 1)
            act.wait_ge(s_spread, 1)
            make_sel(0)
            for f in range(2):
                for c in range(NCH):
                    n = f * NCH + c
                    if c == 0:
                        if f == 0:
                            piece_hi(0)
                            pro_hi(n)
                            for k in range(1, 6):
                                piece_hi(k)
                            pro_sil(n)
                            for k in range(6, PRE):
                                piece_hi(k)
                            for u in range(LEAD):
                                silu_unit(u, n)
                            for k in range(1, SP):
                                make_sel(k)
                            pro_cwT(n)
                    for u in range(UNITS):
                        if c or u >= LEAD:
                            silu_unit(u, n)
                        if n == 0 and u % 2 == 0 and PRE + u // 2 < 2 * WP:
                            piece_hi(PRE + u // 2)
                        if u or c:
                            hi_unit(*((u - 1, n) if u else (UNITS - 1, n - 1)))
                        if c + 1 < NCH:
                            if u == 12:
                                pro_hi(n + 1)
                            if u == 18:
                                pro_sil(n + 1)
                            if u == 31:
                                pro_cwT(n + 1)
                        if c:
                            if u == 5:
                                epi_y(n - 1)
                            if f == 0 and u == 21:
                                epi_hi(c - 1)
                            if f == 0 and u in (25, 29, 32)[:1 if c == NCH - 1 else 3]:
                                epi_proj_hi(c - 1, (25, 29, 32).index(u))
                    if c == NCH - 1:
                        hi_unit(UNITS - 1, n)
                        if f == 0:
                            epi_proj_hi(c - 1, 1)
                        epi_y(n)
                        if f == 0:
                            epi_proj_hi(c - 1, 2)
                            epi_hi(c)
                            epi_proj_hi(c, 0)
                            epi_proj_hi(c, 1)
                if f == 0:
                    def exp_bank(t, j):
                        if j == 0:
                            act.wait_ge(a_mx, t + 1)
                        if t:
                            act.wait_ge(a_t, KB * (t - 1) + j + 1)
                        nc.scalar.activation(prow[:, j * CH:(j + 1) * CH], lrow[:, j * CH:(j + 1) * CH], ACT.Exp,
                                             bias=nmax[:, t % 2:t % 2 + 1], accum_out=psums[:, t, j:j + 1]).then_inc(a_exp, 1)

                    def turn_hi(t, q):
                        act.wait_ge(a_t, 4 * t + q + 1)
                        if t // GT >= 2 and t % GT == 0 and q == 0:
                            act.wait_ge(a_o, t // GT - 1)
                        nc.scalar.copy(pT[0][:, t // GT % 2, 4 * q:4 * q + 4, t % GT * P:(t % GT + 1) * P],
                                       tb[q % 2][:, :].rearrange("p (k n) -> p k n", n=P)).then_inc(a_thi, 1)

                    def o_copy(g):
                        act.wait_ge(a_o, g + 1)
                        if g:
                            act.wait_ge(a_oT, g)
                        nc.scalar.copy(oT[:, :], ob[g % 2][:, 0:GW]).then_inc(a_oc, 1)

                    for t in range(NT):
                        if t == T_XT:
                            pro_hi(NCH)
                        exp_bank(t, 0)
                        exp_bank(t, 1)
                        turn_hi(t, 0)
                        if t % GT == 0 and t // GT >= 2:
                            o_copy(t // GT - 2)
                        exp_bank(t, 2)
                        turn_hi(t, 1)
                        exp_bank(t, 3)
                        turn_hi(t, 2)
                        turn_hi(t, 3)
                        if t == 0:
                            epi_proj_hi(NCH - 1, 2)
                    pro_sil(NCH)
                    o_copy(NQ - 2)
                    for k in range(SP):
                        make_sel(k)
                    o_copy(NQ - 1)
                    for u in range(LEAD):
                        silu_unit(u, NCH)
                    pro_cwT(NCH)

        @block.vector
        def _(dve):
            steps = [0]

            def link(ins):
                steps[0] += 1
                ins.then_inc(s_dve, 1)
                dve.wait_ge(s_dve, steps[0])

            def gate_unit(u, n):
                U = n * UNITS + u
                dve.wait_ge(s_silu, U + 1)
                if U >= NG:
                    dve.wait_ge(s_ghi, U - NG + 1)
                    wait_low(dve, U - NG)
                if u == 0:
                    nc.vector.tensor_copy(gated[0:F, U % NG, :], silu[0:F, U % NS, :]).then_inc(s_gated, 1)
                    return
                if u in BY_DMA:
                    G = n * ND + BY_DMA.index(u)
                    dve.wait_ge(s_wide[G % NB], 32 * (G // NB + 1))
                    g = wide[:, G % NB, :]
                else:
                    R = n * NP + BY_PE.index(u)
                    dve.wait_ge(s_gate, R + 1)
                    g = gate[R % 2]
                nc.vector.tensor_tensor(gated[:, U % NG, :], silu[:, U % NS, :], g, ALU.mult).then_inc(s_gated, 1)

            def lo_unit(u, n):
                if not on_pool(u):
                    low_part(nc.vector, n * UNITS + u).then_inc(s_glo, 1)

            def raw_stats(k, c, tiles):
                for i in tiles:
                    ins = nc.vector.bn_stats(stat[:, k, i, :], x[:, c * TPC + i, :])
                return ins

            def stats(k, c, done, tiles=range(TPC)):
                link(raw_stats(k, c, tiles))
                for i in range(TPC):
                    ins = nc.vector.bn_aggr(mv[:, k, i, :], stat[:, k, i, :])
                ins.then_inc(done, 1)

            def normed(k, n, c, dst, ready, done, tiles=range(TPC)):
                if 0 in tiles:
                    dve.wait_ge(ready, n + 1)
                    ve, y, t, r = (rs[:, k, i, :] for i in range(4))
                    link(nc.vector.tensor_tensor(t, y, ve, ALU.mult))
                    link(nc.vector.scalar_tensor_tensor(out=t, in0=t, scalar=-0.5, in1=y, op0=ALU.mult, op1=ALU.mult))
                    link(nc.vector.scalar_tensor_tensor(out=r, in0=t, scalar=1.5, in1=y, op0=ALU.add, op1=ALU.mult))
                for i in tiles:
                    nc.vector.tensor_scalar(dst[:, i, :], x[:, c * TPC + i, :], mv[:, k, i, 0:1],
                                            rs[:, k, 3, i:i + 1], ALU.subtract, ALU.mult).then_inc(done, 1)

            def pro_lo(n):
                dve.wait_ge(p_hi, n + 1)
                hi, lo = (a[:, n % 2, :] for a in xnT[n // NCH])
                nc.vector.tensor_tensor(lo, mp[:, :], hi.bitcast(F32), ALU.subtract).then_inc(p_lo, 1)

            def bc(ap):
                return ap.unsqueeze(1).to_broadcast([P, TPC, E])

            def pro_aff(n, step):
                f = n // NCH
                ps = mp[:, 0:TPC * E].rearrange("p (t e) -> p t e", e=E)
                if step == 0:
                    dve.wait_ge(p_aff, n + 1)
                    link(nc.vector.tensor_scalar(rec[:, :, :], ps, 0.0, 2 * TINY, ALU.is_ge, ALU.mult))
                    nc.vector.scalar_tensor_tensor(out=aff[f][:, :, :], in0=ps, scalar=TINY, in1=rec[:, :, :],
                                                   op0=ALU.subtract, op1=ALU.add).then_inc(p_affs, 1)
                else:
                    nc.vector.tensor_tensor(biased[f][:, :, :], ps, bc(bias[:, :]), ALU.add).then_inc(p_bias, 1)

            def pro_top(n, step):
                b = biased[n // NCH]
                if step == 0:
                    dve.wait_ge(p_affs, n + 1)
                    nc.vector.reciprocal(rec[:, :, :], aff[n // NCH][:, :, :])
                if step == 1:
                    dve.wait_ge(p_bias, n + 1)
                    for i in range(TPC):
                        ins = nc.vector.max(top[:, i, :], b[:, i, :])
                    ins.then_inc(p_max, 1)
                if step == 2:
                    dve.wait_ge(p_max, n + 1)
                    for i in range(TPC):
                        ins = nc.vector.match_replace(rest[:, i, :], top[:, i, :], b[:, i, :], LOWEST)
                    link(ins)
                    nc.vector.tensor_tensor(rest[:, :, :], rest[:, :, :], b[:, :, :], ALU.not_equal).then_inc(p_top, 1)

            def first_weights(n):
                dve.wait_ge(p_sil, n + 1)
                dve.wait_ge(p_top, n + 1)
                link(nc.vector.tensor_tensor(rec[:, :, :], rec[:, :, :], sil[:, :, :], ALU.mult))
                nc.vector.tensor_tensor(rec[:, :, :], rec[:, :, :], rest[:, :, :], ALU.mult).then_inc(p_w, 1)
                pro_sum(n)
                dve.wait_ge(p_inv, n + 1)
                inv = wsum[:, 1, :].unsqueeze(2).to_broadcast([P, TPC, E])
                nc.vector.tensor_tensor(rest[:, :, :].bitcast(F32R), rec[:, :, :], inv, ALU.mult)
                link(nc.vector.tensor_tensor(cw2[:, :, 0:E], rec[:, :, :], inv, ALU.mult))
                nc.vector.tensor_tensor(cw2[:, :, E:2 * E], cw2[:, :, 0:E], rest[:, :, :], ALU.subtract).then_inc(p_cw, 1)

            def pro_sum(n):
                dve.wait_ge(p_w, n + 1)
                link(nc.vector.tensor_reduce(wsum[:, 0, :], rec[:, :, :], AX, ALU.add))
                link(nc.vector.tensor_scalar(wsum[:, 0, :], wsum[:, 0, :], 1e-8, None, ALU.add))
                nc.vector.reciprocal(wsum[:, 1, :], wsum[:, 0, :]).then_inc(p_inv, 1)

            def epi_x(n, c):
                dve.wait_ge(e_yT, n + 1)
                nc.vector.tensor_tensor(x[:, c * TPC:(c + 1) * TPC, :], x[:, c * TPC:(c + 1) * TPC, :],
                                        mq[:, :].rearrange("p (t d) -> p t d", d=D), ALU.add).then_inc(e_x, 1)

            def epi_lo(c):
                dve.wait_ge(e_hi, c + 1)
                nc.vector.tensor_tensor(x2T[1][:, :], mq[:, :], x2T[0][:, :].bitcast(F32), ALU.subtract).then_inc(e_lo, 1)

            def epi_proj_lo(c, k):
                dve.wait_ge(e_prhi, 3 * c + k + 1)
                dst = proj_parts(c, k)
                nc.vector.tensor_tensor(dst[1], proj_bank(c, k), dst[0].bitcast(F32), ALU.subtract).then_inc(e_prlo, 1)

            def epi_stats(c):
                dve.wait_ge(e_x, c + 1)
                stats(1, c, e_st)

            def max_bank(t, j):
                dve.wait_ge(a_l, KB * t + j + 1)
                return nc.vector.reduce_max(pmax[:, j:j + 1], lrow[:, j * CH:(j + 1) * CH], AX)

            def row_max(t):
                if t >= 2:
                    dve.wait_ge(a_exp, KB * (t - 1))
                nc.vector.tensor_reduce(nmax[:, t % 2:t % 2 + 1], pmax[:, :], AX, ALU.max, negate=True).then_inc(a_mx, 1)

            dve.wait_ge(s_x[0], 16)
            stats(0, 0, p_st)
            dve.wait_ge(s_id, 1)
            nc.vector.tensor_tensor(spread[:, :], ident[:, 0:E], ident[:, E:2 * E], ALU.add).then_inc(s_spread, 1)
            for f in range(2):
                for c in range(NCH):
                    n = f * NCH + c
                    if c == 0:
                        if f == 0:
                            normed(0, n, 0, xn[f], p_rs, p_xn)
                            dve.wait_ge(s_wh, 2)
                            for parts, whole in ((small, raws), (wsdn, rawd)):
                                nc.vector.tensor_tensor(parts[1][:, :], whole[:, :], parts[0][:, :].bitcast(F32),
                                                        ALU.subtract).then_inc(s_wl, 1)
                            dve.wait_ge(s_bias, 16)
                            pro_lo(n)
                            pro_aff(n, 0)
                            pro_aff(n, 1)
                            for step in range(3):
                                pro_top(n, step)
                            first_weights(n)
                    for u in range(UNITS):
                        gate_unit(u, n)
                        if u or c:
                            lo_unit(*((u - 1, n) if u else (UNITS - 1, n - 1)))
                        if c + 1 < NCH:
                            if u == 0:
                                if f == 0:
                                    dve.wait_ge(s_x[c + 1], 16)
                                raw_stats(0, c + 1, (0, 1))
                            if u == 2:
                                stats(0, c + 1, p_st, (2, 3))
                            if u == 6:
                                normed(0, n + 1, c + 1, xn[f], p_rs, p_xn, (0, 1))
                            if u == 8:
                                normed(0, n + 1, c + 1, xn[f], p_rs, p_xn, (2, 3))
                            if u == 12:
                                pro_lo(n + 1)
                            if u == 15:
                                pro_aff(n + 1, 0)
                            if u == 16:
                                pro_aff(n + 1, 1)
                            if u == 18:
                                pro_top(n + 1, 0)
                            if u == 20:
                                pro_top(n + 1, 1)
                            if u == 22:
                                pro_top(n + 1, 2)
                            if u == 24:
                                pro_sum(n + 1)
                        if c:
                            if u == 9:
                                epi_x(n - 1, c - 1)
                            if f == 0:
                                if u == 10:
                                    epi_stats(c - 1)
                                if u == 16:
                                    normed(1, c - 1, c - 1, xn2, e_rs, e_xn, (0, 1))
                                if u == 17:
                                    normed(1, c - 1, c - 1, xn2, e_rs, e_xn, (2, 3))
                                if u == 21:
                                    epi_lo(c - 1)
                                if u in (25, 29, 32)[:1 if c == NCH - 1 else 3]:
                                    epi_proj_lo(c - 1, (25, 29, 32).index(u))
                    if c == NCH - 1:
                        lo_unit(UNITS - 1, n)
                        if f == 0:
                            epi_proj_lo(c - 1, 1)
                        epi_x(n, c)
                        if f == 0:
                            epi_stats(c)
                            max_bank(0, 0)
                            max_bank(0, 1)
                            normed(1, c, c, xn2, e_rs, e_xn)
                            max_bank(0, 2)
                            epi_proj_lo(c - 1, 2)
                            epi_lo(c)
                            epi_proj_lo(c, 0)
                            epi_proj_lo(c, 1)
                            link(max_bank(0, KB - 1))
                            row_max(0)
                if f == 0:
                    def turn_lo(t, q):
                        dve.wait_ge(a_thi, 4 * t + q + 1)
                        at = (slice(None), t // GT % 2, slice(4 * q, 4 * q + 4), slice(t % GT * P, (t % GT + 1) * P))
                        nc.vector.tensor_tensor(pT[1][at], tb[q % 2][:, :].rearrange("p (k n) -> p k n", n=P),
                                                pT[0][at].bitcast(F32), ALU.subtract).then_inc(a_tlo, 1)

                    def inverse(g):
                        link(nc.vector.tensor_reduce(pinv[:, g % 2, :, 0], psums[:, GT * g:GT * (g + 1), :], AX, ALU.add))
                        link(nc.vector.reciprocal(pinv[:, g % 2, :, 1], pinv[:, g % 2, :, 0]))
                        link(nc.vector.tensor_scalar(pinv[:, g % 2, :, 0], pinv[:, g % 2, :, 1], NORM, None, ALU.mult))

                    def add_o(g):
                        dve.wait_ge(a_oT, g + 1)
                        inverse(g)
                        for i in range(GT):
                            ins = nc.vector.scalar_tensor_tensor(
                                out=x[:, GT * g + i, :], in0=ob[g % 2][:, GW + i * P:GW + (i + 1) * P],
                                scalar=pinv[:, g % 2, i, 0:1], in1=x[:, GT * g + i, :], op0=ALU.mult, op1=ALU.add)
                        ins.then_inc(a_x, 1)

                    for t in range(NT):
                        if t == T_XT:
                            normed(0, NCH, 0, xn[1], p_rs, p_xn)
                        for j in range(KB):
                            if t and j < KB - 1:
                                turn_lo(t - 1, j)
                                max_bank(t, j)
                        if t:
                            link(max_bank(t, KB - 1))
                            row_max(t)
                            turn_lo(t - 1, KB - 1)
                        if t == 1:
                            epi_proj_lo(NCH - 1, 2)
                        if t % GT == 1 and t // GT >= 2:
                            add_o(t // GT - 2)
                        if t == T_XT - 2:
                            stats(0, 0, p_st)
                        if t == T_XT:
                            pro_lo(NCH)
                        if t == T_AFF:
                            pro_aff(NCH, 0)
                            pro_aff(NCH, 1)
                        if t > T_AFF:
                            pro_top(NCH, t - T_AFF - 1)
                    for j in range(KB):
                        turn_lo(NT - 1, j)
                        if j == 1:
                            pro_top(NCH, 2)
                    first_weights(NCH)
                    add_o(NQ - 2)
                    add_o(NQ - 1)
                    dve.wait_ge(a_x, NQ)

        @block.tensor
        def _(pe):
            def product(out, a, b):
                nc.tensor.matmul(out, a[0], b[1], start=True, stop=False)
                nc.tensor.matmul(out, a[1], b[0], start=False, stop=False)
                return nc.tensor.matmul(out, a[0], b[0], start=False, stop=True)

            def up(u, n):
                U = n * UNITS + u
                if n == 0 and u and (u - 1) % (PAIRS // WP) == 0:
                    pe.wait_ge(s_w, 2 * ((u - 1) // (PAIRS // WP)) + 1)
                if U >= 2:
                    pe.wait_ge(s_silu, U - 1)
                w = [a[:, (u - 1) * P:u * P] for a in wup] if u else wsup
                product(hid[U % 2][0:P if u else F, :], w, [a[:, n % 2, :] for a in xnT[n // NCH]]).then_inc(s_hid, 1)

            def spread_gate(u, n):
                if u in BY_PE:
                    i = BY_PE.index(u)
                    R = n * NP + i
                    if R >= 2:
                        pe.wait_ge(s_gated, pe_unit(R - 2) + 1)
                    if n % NCH == 0 and i in (0, FIRST_DMA - 1):
                        pe.wait_ge(s_sel, n // NCH * SP + (1 if i == 0 else 2))
                    one = sel[:, i, :, :].rearrange("p e f -> p (e f)")
                    nc.tensor.matmul(gate[R % 2], one, cwT[n // NCH][n % 2][:, :], start=True, stop=True).then_inc(s_gate, 1)

            def down(u, n):
                U = n * UNITS + u
                m = P if u else F
                if n == 0 and u and (u - 1) % (PAIRS // WP) == 0:
                    pe.wait_ge(s_w, 2 * ((u - 1) // (PAIRS // WP)) + 2)
                if u == 0 and n % NCH >= 2:
                    pe.wait_ge(e_y, n - 1)
                wait_low(pe, U)
                w = [a[:, u - 1, :] for a in wdn] if u else [a[:, :] for a in wsdn]
                g = [a[0:m, U % NGP, :] for a in gpart]
                y = yacc[n % 2][:, :]
                nc.tensor.matmul(y, w[0], g[1], start=(u == 0), stop=False)
                nc.tensor.matmul(y, w[1], g[0], start=False, stop=False)
                nc.tensor.matmul(y, w[0], g[0], start=False, stop=(u == UNITS - 1)).then_inc(s_down, 1)

            def turn(src, ps, done):
                for i in range(TPC):
                    ins = nc.tensor.transpose(ps[:, i * P:(i + 1) * P], src[:, i * P:(i + 1) * P], ident[:, :])
                ins.then_inc(done, 1)

            def turn_tiles(src, ps, ready, n, done):
                for i in range(TPC):
                    pe.wait_ge(ready, TPC * n + i + 1)
                    ins = nc.tensor.transpose(ps[:, i * P:(i + 1) * P], src[:, i, :], ident[:, :])
                ins.then_inc(done, 1)

            def pro_xT(n):
                if n:
                    pe.wait_ge(s_gates, n)
                turn_tiles(xn[n // NCH], mp, p_xn, n, p_xT)

            def pro_aff(n):
                pe.wait_ge(p_lo, n + 1)
                for i in range(TPC):
                    ins = product(mp[:, i * E:(i + 1) * E], [a[:, n % 2, i * P:(i + 1) * P] for a in xnT[n // NCH]], cen)
                ins.then_inc(p_aff, 1)

            def pro_cw(n):
                pe.wait_ge(p_cw, n + 1)
                turn(flat(cw2), mp, p_cwT)

            def epi_yT(n):
                pe.wait_ge(e_y, n + 1)
                if 0 < n <= NCH:
                    pe.wait_ge(e_prlo, 3 * n - 2 if n == NCH - 1 else 3 * n)
                elif n:
                    pe.wait_ge(e_x, n)
                turn(yT, mq, e_yT)

            def epi_xT(c):
                turn_tiles(xn2, mq, e_xn, c, e_xT)

            def epi_proj(c, k):
                if k == 0:
                    pe.wait_ge(e_lo, c + 1)
                elif c < NCH - 2:
                    pe.wait_ge(e_prlo, 3 * c + k)
                out = proj_bank(c, k)
                if k < 2:
                    ins = product(out, (wk, wq)[k], [a[:, :] for a in x2T])
                else:
                    for i in range(TPC):
                        ins = product(out[:, i * D:(i + 1) * D], [a[:, i * P:(i + 1) * P] for a in x2T], wv)
                ins.then_inc(e_pr, 1)

            def logits(t, j):
                if t:
                    pe.wait_ge(a_exp, KB * (t - 1) + j + 1)
                product(lrow[:, j * CH:(j + 1) * CH], [a[:, t * P:(t + 1) * P] for a in qT],
                        [a[:, j * CH:(j + 1) * CH] for a in kT]).then_inc(a_l, 1)

            pe.wait_ge(s_id, 1)
            for f in range(2):
                for c in range(NCH):
                    n = f * NCH + c
                    if n == 0:
                        pro_xT(n)
                        pe.wait_ge(s_wl, 2)
                        pro_aff(n)
                        for u in range(LEAD):
                            up(u, n)
                        pro_cw(n)
                    pe.wait_ge(p_cwr, n + 1)
                    for u in range(UNITS):
                        if c or u >= LEAD:
                            up(u, n)
                        spread_gate(u, n)
                        if u >= LAG:
                            down(u - LAG, n)
                        elif c:
                            down(UNITS - LAG + u, n - 1)
                        if c + 1 < NCH:
                            if u == 11:
                                pro_xT(n + 1)
                            if u == 14:
                                pro_aff(n + 1)
                            if u == 30:
                                pro_cw(n + 1)
                        if c:
                            if u == 8:
                                epi_yT(n - 1)
                            if f == 0:
                                if u == 20:
                                    epi_xT(c - 1)
                                if u in (24, 28, 31)[:1 if c == NCH - 1 else 3]:
                                    epi_proj(c - 1, (24, 28, 31).index(u))
                    if c == NCH - 1:
                        for u in range(UNITS - LAG, UNITS):
                            down(u, n)
                            if f == 0 and u == UNITS - LAG:
                                epi_proj(c - 1, 1)
                        if f == 0:
                            pe.wait_ge(e_prlo, 3 * c - 2)
                            logits(0, 0)
                            logits(0, 1)
                        epi_yT(n)
                        if f == 0:
                            logits(0, 2)
                            epi_proj(c - 1, 2)
                            epi_xT(c)
                            epi_proj(c, 0)
                            epi_proj(c, 1)
                            pe.wait_ge(e_prlo, 3 * c + 1)
                            logits(0, KB - 1)
                            epi_proj(c, 2)
                if f == 0:
                    def turn_p(t, q):
                        pe.wait_ge(a_exp, KB * t + q + 1)
                        if 4 * t + q >= 2:
                            pe.wait_ge(a_tlo, 4 * t + q - 1)
                        if q == 0 and t == T_XT:
                            pe.wait_ge(p_lo, NCH + 1)
                        if q == 0 and t == T_AFF:
                            pe.wait_ge(p_bias, NCH + 1)
                        turn(prow[:, q * CH:(q + 1) * CH], tb[q % 2], a_t)

                    def weigh(g, ks):
                        for k in ks:
                            if k == 0 and g == 0:
                                pe.wait_ge(e_prlo, 3 * NCH)
                            if k == 0 and g >= 2:
                                pe.wait_ge(a_x, g - 1)
                            if k % 4 == 0:
                                pe.wait_ge(a_tlo, 4 * (GT * g + GT - 1) + k // 4 + 1)
                            p = [a[:, g % 2, k, :] for a in pT]
                            o = ob[g % 2][:, 0:GW]
                            nc.tensor.matmul(o, v[0][:, k, :], p[1], start=(k == 0), stop=False)
                            nc.tensor.matmul(o, v[1][:, k, :], p[0], start=False, stop=False)
                            ins = nc.tensor.matmul(o, v[0][:, k, :], p[0], start=False, stop=(k == NT - 1))
                            if k == NT - 1:
                                ins.then_inc(a_o, 1)

                    def turn_o(g):
                        pe.wait_ge(a_oc, g + 1)
                        for i in range(GT):
                            ins = nc.tensor.transpose(ob[g % 2][:, GW + i * P:GW + (i + 1) * P],
                                                      oT[:, i * P:(i + 1) * P], ident[:, :])
                        ins.then_inc(a_oT, 1)

                    pe.wait_ge(e_prlo, 3 * NCH - 3)
                    half = NT // GT
                    for t in range(NT):
                        g = t // GT
                        at = t % GT * half
                        for j, n_k in enumerate(SHARE):
                            if t:
                                turn_p(t - 1, j)
                                logits(t, j)
                            if j == KB - 1:
                                if t % GT == 1 and g >= 2:
                                    turn_o(g - 2)
                                if t == T_XT:
                                    pe.wait_ge(a_tlo, 4 * (t - 1) + 3)
                                    pro_xT(NCH)
                                if t == T_AFF:
                                    pe.wait_ge(a_tlo, 4 * (t - 1) + 3)
                                    pro_aff(NCH)
                            if g:
                                weigh(g - 1, range(at, at + n_k))
                                at += n_k
                    for j in range(KB):
                        turn_p(NT - 1, j)
                    weigh(NQ - 1, range(NT))
                    turn_o(NQ - 2)
                    for u in range(LEAD):
                        up(u, NCH)
                        if u == 1:
                            turn_o(NQ - 1)
                    pro_cw(NCH)


def kernel(L0_attn_x, L0_attn_Wq, L0_attn_Wk, L0_attn_Wv, L0_ffn_centroids, L0_ffn_expert_biases,
           L0_ffn_Ws_up, L0_ffn_Ws_down, L0_ffn_W_up, L0_ffn_W_down):
    import numpy as np
    import concourse.bacc as bacc
    from concourse.bass_utils import run_bass_kernel_spmd as run

    x = np.asarray(L0_attn_x)
    b, s, d = x.shape
    w_up, w_down = np.asarray(L0_ffn_W_up), np.asarray(L0_ffn_W_down)
    e, _, f = w_up.shape
    arrays = {
        "x": x.reshape(b * s, d),
        "w_up": w_up.transpose(1, 0, 2).reshape(d, e * f),
        "w_down": w_down.reshape(e // 2, 2 * f, d).transpose(1, 0, 2).reshape(2 * f, e // 2 * d),
        "ws_up": np.asarray(L0_ffn_Ws_up),
        "ws_down": np.asarray(L0_ffn_Ws_down),
        "centroids": np.asarray(L0_ffn_centroids).T,
        "biases": np.asarray(L0_ffn_expert_biases),
        "wq": np.asarray(L0_attn_Wq).T,
        "wk": np.asarray(L0_attn_Wk).T,
        "wv": np.asarray(L0_attn_Wv).T,
    }
    arrays = {n: np.ascontiguousarray(a) for n, a in arrays.items()}
    nc = bacc.Bacc("TRN2", target_bir_lowering=False, num_devices=1)
    args = [nc.dram_tensor("in_" + n, a.shape, mybir.dt.from_np(a.dtype), kind="ExternalInput").ap() for n, a in arrays.items()]
    gates = nc.dram_tensor("gates_dram", (2 * (b * s // CH), e, CH), F32, kind="Internal").ap()
    out = nc.dram_tensor("out_dram", (b * s, d), F32, kind="ExternalOutput").ap()
    macaron_kernel(nc, *args, gates, out)
    r = run(nc, [{"in_" + n: a for n, a in arrays.items()}], core_ids=[0])
    return r.results[0]["out_dram"].reshape(b, s, d)
```
